# Optimizing a Trainium2 kernel written in Bass

```python
import numpy as np
import jax
import jax.numpy as jnp

def _softmax(x, axis=-1):
    return jax.nn.softmax(x, axis=axis)

def _gelu(x):
    return jax.nn.gelu(x, approximate=True)

def _silu(x):
    return jax.nn.silu(x)

def _sigmoid(x):
    return jax.nn.sigmoid(x)

def _layernorm(x, axis=-1, eps=1e-05):
    m = jnp.mean(x, axis=axis, keepdims=True)
    v = jnp.var(x, axis=axis, keepdims=True)
    return (x - m) / jnp.sqrt(v + eps)

def _scatter_add(tgt, idx, src, axis=0):
    return tgt.at[idx].add(src)

def _segment_sum(src, seg, n):
    return jax.ops.segment_sum(src, seg, n)
kernel_name = 'mk_adaln_ffn_d2_seqx_r8_f55455'

def setup_inputs(seed: int=0):
    np.random.seed(seed)
    _w = jnp.asarray

    def _rec_inputs():
        import jax
        import jax.numpy as jnp
        _rk = jax.random.key(seed)
        x = -7.109e-05 + 0.9999 * jax.random.normal(jax.random.fold_in(_rk, 1), (64, 32, 128), jnp.float32)
        _lenS = 32 - jax.random.randint(jax.random.fold_in(_rk, 7), (64,), 0, max(1, 32 // 4) + 1, jnp.int32)
        _lenS2 = 32 - jax.random.randint(jax.random.fold_in(_rk, 8), (64,), 0, max(1, 32 // 4) + 1, jnp.int32)
        cond_1024 = -0.00356592 + 0.997978 * jax.random.normal(jax.random.fold_in(_rk, 11), (64, 128), jnp.float32)
        return (x, cond_1024)
    x, cond_1024 = _rec_inputs()

    def _L0_cond_setup():
        import jax, jax.numpy as jnp
        import numpy as np
        N, T, D, H = (128, 64, 128, 128)
        key = jax.random.key(seed)
        k1, k2, k3, k4 = jax.random.split(key, 4)
        x = jax.random.normal(k1, (N, T, D), dtype=jnp.float32)
        h0 = jax.random.normal(k2, (N, H), dtype=jnp.float32)
        Wx = jax.random.normal(k3, (D, H), dtype=jnp.float32) / np.sqrt(D)
        Wh = jax.random.normal(k4, (H, H), dtype=jnp.float32) / np.sqrt(H)
        b = jnp.zeros((H,), dtype=jnp.float32)
        return {'x': x, 'h0': h0, 'Wx': Wx, 'Wh': Wh, 'b': b}
    _L0_cond_all = _L0_cond_setup()
    _L0_cond_in = {k: v for k, v in _L0_cond_all.items() if k in ('Wx', 'Wh', 'b')}
    del _L0_cond_all

    def _L0_ffn_setup():
        import jax, jax.numpy as jnp
        import numpy as np
        B, S, DIM = (4, 256, 128)
        INTER = int(int(DIM * 4) * 0.25)
        E = 32 - 1
        K = 4 - 1

        def _gelu(t):
            return jax.nn.gelu(t, approximate=False)
        key = jax.random.key(seed)
        ks = jax.random.split(key, 12)
        s = 0.02
        return {'x': jax.random.normal(ks[0], (B, S, DIM), jnp.float32), 'ws1': jax.random.normal(ks[1], (DIM, INTER), jnp.float32) * s, 'bs1': jnp.zeros((INTER,), jnp.float32), 'ws2': jax.random.normal(ks[2], (INTER, DIM), jnp.float32) * s, 'bs2': jnp.zeros((DIM,), jnp.float32), 'We1': jax.random.normal(ks[3], (E, DIM, INTER), jnp.float32) * s, 'Be1': jnp.zeros((E, INTER), jnp.float32), 'We2': jax.random.normal(ks[4], (E, INTER, DIM), jnp.float32) * s, 'Be2': jnp.zeros((E, DIM), jnp.float32), 'Wr': jax.random.normal(ks[5], (DIM, E), jnp.float32) * s, 'br': jnp.zeros((E,), jnp.float32)}
    _L0_ffn_all = _L0_ffn_setup()
    _L0_ffn_in = {k: v for k, v in _L0_ffn_all.items() if k in ('ws1', 'bs1', 'ws2', 'bs2', 'We1', 'Be1', 'We2', 'Be2', 'Wr', 'br')}
    del _L0_ffn_all

    def _L1_cond_setup():
        import jax, jax.numpy as jnp
        import numpy as np
        NUM_EXPERTS = 4
        TOP_K = 2
        key = jax.random.key(seed)
        ks = jax.random.split(key, 16)
        B, L, D, E, H = (8, 96, 128, NUM_EXPERTS, 512)
        s = 0.02
        return {'context_c': jax.random.normal(ks[0], (B, L, D), jnp.float32), 'time_cond': jax.random.normal(ks[1], (B, D), jnp.float32), 'gate_w': jax.random.normal(ks[2], (3 * D, E), jnp.float32) * s, 'gate_b': jnp.zeros((E,), jnp.float32), 'time_w': jax.random.normal(ks[3], (D, 2 * E), jnp.float32) * s, 'time_b': jnp.zeros((2 * E,), jnp.float32), 'ew1': jax.random.normal(ks[4], (E, D, H), jnp.float32) * s, 'eb1': jnp.zeros((E, H), jnp.float32), 'ew2': jax.random.normal(ks[5], (E, H, D), jnp.float32) * s, 'eb2': jnp.zeros((E, D), jnp.float32), 'sw1': jax.random.normal(ks[6], (D, H), jnp.float32) * s, 'sb1': jnp.zeros((H,), jnp.float32), 'sw2': jax.random.normal(ks[7], (H, D), jnp.float32) * s, 'sb2': jnp.zeros((D,), jnp.float32)}
    _L1_cond_all = _L1_cond_setup()
    _L1_cond_in = {k: v for k, v in _L1_cond_all.items() if k in ('gate_w', 'gate_b', 'time_w', 'time_b', 'ew1', 'eb1', 'ew2', 'eb2', 'sw1', 'sb1', 'sw2', 'sb2')}
    del _L1_cond_all

    def _L1_ffn_setup():
        import jax, jax.numpy as jnp
        import numpy as np
        TEMPERATURE = 1.0
        TOPK = 2
        key = jax.random.key(seed)
        ks = jax.random.split(key, 6)
        S, B, H, F, E = (256, 4, 128, 512, 8)
        x = jax.random.normal(ks[0], (S, B, H), dtype=jnp.float32)
        gate_w = jax.random.normal(ks[1], (E, H), dtype=jnp.float32) * (1.0 / np.sqrt(H))
        w1 = jax.random.normal(ks[2], (E, H, F), dtype=jnp.float32) * (1.0 / np.sqrt(H))
        b1 = jnp.zeros((E, F), dtype=jnp.float32)
        w2 = jax.random.normal(ks[3], (E, F, H), dtype=jnp.float32) * (1.0 / np.sqrt(F))
        b2 = jnp.zeros((E, H), dtype=jnp.float32)
        return {'x': x, 'gate_w': gate_w, 'w1': w1, 'b1': b1, 'w2': w2, 'b2': b2}
    _L1_ffn_all = _L1_ffn_setup()
    _L1_ffn_in = {k: v for k, v in _L1_ffn_all.items() if k in ('gate_w', 'w1', 'b1', 'w2', 'b2')}
    del _L1_ffn_all
    return {'x': x, 'cond_1024': cond_1024, 'L0_cond_Wx': _L0_cond_in['Wx'], 'L0_cond_Wh': _L0_cond_in['Wh'], 'L0_cond_b': _L0_cond_in['b'], 'L0_ffn_ws1': _L0_ffn_in['ws1'], 'L0_ffn_bs1': _L0_ffn_in['bs1'], 'L0_ffn_ws2': _L0_ffn_in['ws2'], 'L0_ffn_bs2': _L0_ffn_in['bs2'], 'L0_ffn_We1': _L0_ffn_in['We1'], 'L0_ffn_Be1': _L0_ffn_in['Be1'], 'L0_ffn_We2': _L0_ffn_in['We2'], 'L0_ffn_Be2': _L0_ffn_in['Be2'], 'L0_ffn_Wr': _L0_ffn_in['Wr'], 'L0_ffn_br': _L0_ffn_in['br'], 'L1_cond_gate_w': _L1_cond_in['gate_w'], 'L1_cond_gate_b': _L1_cond_in['gate_b'], 'L1_cond_time_w': _L1_cond_in['time_w'], 'L1_cond_time_b': _L1_cond_in['time_b'], 'L1_cond_ew1': _L1_cond_in['ew1'], 'L1_cond_eb1': _L1_cond_in['eb1'], 'L1_cond_ew2': _L1_cond_in['ew2'], 'L1_cond_eb2': _L1_cond_in['eb2'], 'L1_cond_sw1': _L1_cond_in['sw1'], 'L1_cond_sb1': _L1_cond_in['sb1'], 'L1_cond_sw2': _L1_cond_in['sw2'], 'L1_cond_sb2': _L1_cond_in['sb2'], 'L1_ffn_gate_w': _L1_ffn_in['gate_w'], 'L1_ffn_w1': _L1_ffn_in['w1'], 'L1_ffn_b1': _L1_ffn_in['b1'], 'L1_ffn_w2': _L1_ffn_in['w2'], 'L1_ffn_b2': _L1_ffn_in['b2']}

def reference(x, cond_1024, L0_cond_Wx, L0_cond_Wh, L0_cond_b, L0_ffn_ws1, L0_ffn_bs1, L0_ffn_ws2, L0_ffn_bs2, L0_ffn_We1, L0_ffn_Be1, L0_ffn_We2, L0_ffn_Be2, L0_ffn_Wr, L0_ffn_br, L1_cond_gate_w, L1_cond_gate_b, L1_cond_time_w, L1_cond_time_b, L1_cond_ew1, L1_cond_eb1, L1_cond_ew2, L1_cond_eb2, L1_cond_sw1, L1_cond_sb1, L1_cond_sw2, L1_cond_sb2, L1_ffn_gate_w, L1_ffn_w1, L1_ffn_b1, L1_ffn_w2, L1_ffn_b2):
    import jax
    import jax.numpy as jnp

    def _L0_cond_ref(x, h0, Wx, Wh, b):
        import jax, jax.numpy as jnp
        import numpy as np
        N, T, D, H = (128, 64, 128, 128)
        xp = jnp.einsum('ntd,dh->nth', x, Wx) + b

        def step(prev_h, xp_t):
            next_h = jnp.tanh(xp_t + prev_h @ Wh)
            return (next_h, next_h)
        _, h = jax.lax.scan(step, h0, jnp.swapaxes(xp, 0, 1))
        return jnp.swapaxes(h, 0, 1)

    def _L0_ffn_ref(x, ws1, bs1, ws2, bs2, We1, Be1, We2, Be2, Wr, br):
        import jax, jax.numpy as jnp
        import numpy as np
        B, S, DIM = (4, 256, 128)
        INTER = int(int(DIM * 4) * 0.25)
        E = 32 - 1
        K = 4 - 1

        def _gelu(t):
            return jax.nn.gelu(t, approximate=False)
        shared = _gelu(x @ ws1 + bs1) @ ws2 + bs2
        aff = jax.nn.softmax(x @ Wr + br, axis=-1)
        vals, idx = jax.lax.top_k(aff, K)
        gates = jnp.sum(jax.nn.one_hot(idx, E, dtype=x.dtype) * vals[..., None], axis=-2)
        gates_e = jnp.moveaxis(gates, -1, 0)

        def step(acc, p):
            W1, B1, W2, B2, g = p
            h = _gelu(x @ W1 + B1)
            return (acc + g[..., None] * (h @ W2 + B2), None)
        routed, _ = jax.lax.scan(step, jnp.zeros_like(x), (We1, Be1, We2, Be2, gates_e))
        return shared + routed + x

    def _L1_cond_ref(context_c, time_cond, gate_w, gate_b, time_w, time_b, ew1, eb1, ew2, eb2, sw1, sb1, sw2, sb2):
        import jax, jax.numpy as jnp
        import numpy as np
        NUM_EXPERTS = 4
        TOP_K = 2
        B, L, D = context_c.shape
        E, K = (NUM_EXPERTS, TOP_K)
        L_head = L_wrist = L // 3
        head = context_c[:, :L_head]
        wrist = context_c[:, L_head:L_head + L_wrist]
        proprio = context_c[:, L_head + L_wrist:]
        full_agg = context_c.mean(axis=1)
        hp_agg = jnp.concatenate([head, proprio], axis=1).mean(axis=1)
        wp_agg = jnp.concatenate([wrist, proprio], axis=1).mean(axis=1)
        gate_in = jnp.concatenate([full_agg, hp_agg, wp_agg], axis=-1)
        gate_logits = gate_in @ gate_w + gate_b
        mod = jax.nn.silu(time_cond) @ time_w + time_b
        scale, shift = jnp.split(mod, 2, axis=-1)
        gate_logits = gate_logits * (1.0 + scale) + shift
        gate_scores = jax.nn.softmax(gate_logits, axis=-1)
        topk_w, topk_i = jax.lax.top_k(gate_scores, K)
        topk_w = topk_w / (topk_w.sum(axis=-1, keepdims=True) + 1e-08)
        onehot = (topk_i[..., None] == jnp.arange(E)[None, None, :]).astype(context_c.dtype)
        w_be = jnp.sum(topk_w[..., None] * onehot, axis=1)
        mask = np.ones((E, L), dtype=np.float32)
        mask[1, L_head:L_head + L_wrist] = 0.0
        mask[2, :L_head] = 0.0
        mask = jnp.asarray(mask)
        out = jnp.zeros_like(context_c)
        for e in range(E):
            h = jax.nn.gelu(context_c @ ew1[e] + eb1[e], approximate=True)
            y = h @ ew2[e] + eb2[e]
            out = out + w_be[:, e][:, None, None] * mask[e][None, :, None] * y
        shared = jax.nn.gelu(context_c @ sw1 + sb1, approximate=True) @ sw2 + sb2
        return out + shared

    def _L1_ffn_ref(x, gate_w, w1, b1, w2, b2):
        import jax, jax.numpy as jnp
        import numpy as np
        TEMPERATURE = 1.0
        TOPK = 2
        s, b, h = x.shape
        x_flat = x.reshape(s * b, h)
        logits = x_flat @ gate_w.T
        probs = jax.nn.softmax(logits / TEMPERATURE, axis=-1)
        topk_probs, topk_idx = jax.lax.top_k(probs, TOPK)
        hidden = jax.nn.relu(jnp.einsum('th,ehf->tef', x_flat, w1) + b1[None])
        all_out = jnp.einsum('tef,efh->teh', hidden, w2) + b2[None]
        gathered = jnp.take_along_axis(all_out, topk_idx[:, :, None], axis=1)
        y_flat = jnp.sum(gathered * topk_probs[:, :, None], axis=1)
        return y_flat.reshape(s, b, h)
    x = x + _L0_ffn_ref(_L0_cond_ref(x, cond_1024, L0_cond_Wx, L0_cond_Wh, L0_cond_b), L0_ffn_ws1, L0_ffn_bs1, L0_ffn_ws2, L0_ffn_bs2, L0_ffn_We1, L0_ffn_Be1, L0_ffn_We2, L0_ffn_Be2, L0_ffn_Wr, L0_ffn_br)
    x = x + _L1_ffn_ref(_L1_cond_ref(x, cond_1024, L1_cond_gate_w, L1_cond_gate_b, L1_cond_time_w, L1_cond_time_b, L1_cond_ew1, L1_cond_eb1, L1_cond_ew2, L1_cond_eb2, L1_cond_sw1, L1_cond_sb1, L1_cond_sw2, L1_cond_sb2), L1_ffn_gate_w, L1_ffn_w1, L1_ffn_b1, L1_ffn_w2, L1_ffn_b2)
    return x

_drawn_inputs = setup_inputs


def setup_inputs(seed=0):
    import zlib

    import numpy as np

    out = dict(_drawn_inputs(seed))
    spreads = {'L0_cond_b': (0.0, 0.1),
     'L0_ffn_bs1': (0.0, 0.781),
     'L0_ffn_bs2': (0.0, 0.1),
     'L0_ffn_Be1': (0.0, 0.8),
     'L0_ffn_Be2': (0.0, 0.8),
     'L0_ffn_br': (0.0, 0.8),
     'L1_cond_gate_b': (0.0, 0.477),
     'L1_cond_time_b': (0.0, 0.777),
     'L1_cond_eb1': (0.0, 0.8),
     'L1_cond_eb2': (0.0, 0.358),
     'L1_cond_sb1': (0.0, 0.757),
     'L1_cond_sb2': (0.0, 0.284),
     'L1_ffn_b1': (0.0, 0.714),
     'L1_ffn_b2': (0.0, 0.454)}
    factors = {'L0_ffn_ws1': 3.686,
     'L0_ffn_ws2': 3.033,
     'L0_ffn_We1': 8.0,
     'L0_ffn_We2': 8.0,
     'L0_ffn_Wr': 8.0,
     'L1_cond_gate_w': 5.094,
     'L1_cond_time_w': 6.033,
     'L1_cond_ew1': 4.148,
     'L1_cond_ew2': 3.952,
     'L1_cond_sw1': 3.313,
     'L1_cond_sw2': 3.191,
     'L1_ffn_w1': 3.669}
    for name, (base, spread) in spreads.items():
        noise = np.random.default_rng([zlib.crc32(name.encode()), seed]).standard_normal(out[name].shape)
        drawn = base * np.exp(spread * noise) if base else spread * noise
        out[name] = jnp.asarray(drawn.astype(out[name].dtype))
    for name, factor in factors.items():
        out[name] = (out[name] * factor).astype(out[name].dtype)
    return out
```

```python
from contextlib import ExitStack

import concourse.bass as bass
from concourse import mybir

ACT = mybir.ActivationFunctionType
ALU = mybir.AluOpType
AX = mybir.AxisListType.X
F32 = mybir.dt.float32
F32R = mybir.dt.float32r
BF16 = mybir.dt.bfloat16

B, T, D = 64, 32, 128
NT = B * T
P = 128
TILES = NT // P
C0 = 512
J0 = NT // C0
C1 = 1024
J1 = NT // C1
E0, K0 = 31, 3
N0 = E0 + 1
EC, KC = 4, 2
NC_ = EC + 1
EF, KF = 8, 2
FC = 4
GW = 32
T_HEAD = T_WRIST = T // 3
NEG = -3.0e38
TAKEN = 3.0e38

R_B0 = 0
R_BC = R_B0 + N0
R_BF = R_BC + NC_ * FC
R_YC = R_BF + EF * FC
R_YF = R_YC + NC_
R_GF = R_YF + EF
ROWS = R_GF + EF

USUAL = [("F", 0, 0), ("F", 0, 1), ("F", 0, 2), ("F", 0, 3), ("G", 0, 0),
         ("F", 1, 0), ("F", 1, 1), ("F", 1, 2), ("F", 1, 3), ("G", 1, 0)]
FIRST_C = [("F", 0, 0), ("F", 0, 1), ("F", 0, 2), ("F", 0, 3), ("A", 0, 0),
           ("F", 1, 0), ("F", 1, 1), ("F", 1, 2), ("F", 1, 3), ("X", 0, 0)]
FIRST_F = [("F", 0, 0), ("F", 0, 1), ("R", 0, 0), ("F", 0, 2), ("F", 0, 3), ("F", 1, 0),
           ("F", 1, 1), ("F", 1, 2), ("X", 0, 0), ("G", 0, 0), ("F", 1, 3), ("G", 1, 0)]
LAG0 = 3
N_SMALL = 21
N_WC = 3 + EC
N_WF = 1 + EF
LAG1 = 2


def build(nc, x, cond, Wx, Wh, rb, ws1, bs1, ws2, bs2, We1, Be1, We2, Be2, Wr, br,
          cgw, cgb, ctw, ctb, ew1, eb1, ew2, eb2, sw1, sb1, sw2, sb2, fgw, fw1, fb1, fw2, fb2, out):
    ctx = ExitStack()
    with ctx:
        def sb(name, shape, dt):
            return ctx.enter_context(nc.sbuf_tensor(name, shape, dt))

        def sem(name):
            return ctx.enter_context(nc.semaphore(name))

        nat = sb("nat", [P, TILES, D], F32)
        c_f = sb("c_f", [P, NT], F32)
        x_f = sb("x_f", [P, NT], F32)
        h_f = sb("h_f", [P, NT], F32)
        in_hi = sb("in_hi", [P, NT], F32R)
        in_lo = sb("in_lo", [P, NT], F32R)
        raw1 = sb("raw1", [P, N0 * D], F32)
        raw2 = sb("raw2", [P, N0 * D], F32)
        rawc1 = sb("rawc1", [P, NC_ * FC * P], F32)
        rawc2 = sb("rawc2", [P, NC_ * FC * P], F32)
        w1h0 = sb("w1h0", [P, 2, D], F32R)
        w1l0 = sb("w1l0", [P, 2, D], F32R)
        w2h0 = sb("w2h0", [P, 2, D], F32R)
        w2l0 = sb("w2l0", [P, 2, D], F32R)
        w1h = sb("w1h", [P, FC * P], F32R)
        w1l = sb("w1l", [P, FC * P], F32R)
        w2h = sb("w2h", [P, FC * P], F32R)
        w2l = sb("w2l", [P, FC * P], F32R)
        hid = sb("hid", [P, 2, C1], F32)
        hid_g = sb("hid_g", [P, 2, C0], F32)
        hid_hi = sb("hid_hi", [P, 4, C1], F32R)
        hid_lo = sb("hid_lo", [P, 4, C1], F32R)
        yg = sb("yg", [P, 2, C1], F32)
        gates_T = sb("gates_T", [3 * GW, NT], BF16)
        gates3 = sb("gates3", [P, TILES, 3 * GW], BF16)
        gates = sb("gates", [P, TILES, GW], F32)
        g_r1 = sb("g_r1", [P, TILES, GW], F32)
        g_r2 = sb("g_r2", [P, TILES, GW], F32)
        pick = sb("pick", [3 * GW, GW, P], BF16)
        ident = sb("ident", [P, P], F32)
        ident_b = sb("ident_b", [P, P], BF16)
        lg0 = sb("lg0", [P, TILES, E0 + 9], F32)
        lgc = sb("lgc", [P, 1, 16], F32)
        lgf = sb("lgf", [P, TILES, 16], F32)
        left = sb("left", [P, TILES, E0 + 9], F32)
        top8 = sb("top8", [P, TILES, 8], F32)
        take8 = sb("take8", [P, TILES, 8], F32)
        take8c = sb("take8c", [P, 1, 8], F32)
        take8f = sb("take8f", [P, TILES, 8], F32)
        ex = sb("ex", [P, TILES, GW], F32)
        taken = sb("taken", [P, TILES, GW], F32)
        ssum = sb("ssum", [P, TILES], F32)
        rsum = sb("rsum", [P, TILES], F32)
        cond_n = sb("cond_n", [B, D], F32)
        cond2 = sb("cond2", [P, 2, B], F32)
        silu_e = sb("silu_e", [P, 2, B], F32)
        silu2 = sb("silu2", [P, 2, B], F32)
        wx = sb("wx", [D, D], F32)
        wh = sb("wh", [D, D], F32)
        rb_c = sb("rb_c", [P, 1], F32)
        wr = sb("wr", [D, E0], F32)
        br_b = sb("br_b", [P, E0], F32)
        rows = sb("rows", [ROWS, P], F32)
        cols = sb("cols", [P, ROWS], F32)
        cgw_s = sb("cgw_s", [P, 3, EC], F32)
        cgb_b = sb("cgb_b", [P, EC], F32)
        ctw_s = sb("ctw_s", [P, 2 * EC], F32)
        ctb_b = sb("ctb_b", [P, 2 * EC], F32)
        mod = sb("mod", [P, 2 * EC], F32)
        agg_s = sb("agg_s", [P, 3, B], F32)
        agg_t = sb("agg_t", [P, 3, B], F32)
        agg = sb("agg", [P, 3, 2, B], F32)
        la = sb("la", [P, EC], F32)
        wsum = sb("wsum", [P, 1], F32)
        wrec = sb("wrec", [P, 1], F32)
        wbe = sb("wbe", [P, EC], F32)
        be2 = sb("be2", [3 * GW, D], F32)
        be2_r1 = sb("be2_r1", [3 * GW, D], F32)
        be2_r2 = sb("be2_r2", [3 * GW, D], F32)
        be2_p = sb("be2_p", [3 * GW, 3, D], BF16)

        bias0_cur = sb("bias0_cur", [P, 2], F32)
        bias_cur = sb("bias_cur", [P, FC], F32)

        ps = ctx.enter_context(nc.psum_tensor("ps", [P, 8, 512], F32))
        bank = lambda n: ps[:, n, :]
        pair = lambda n: ps[:, n:n + 2, :].rearrange("p a b -> p (a b)")
        GT_BANK = ps[0:3 * GW, 6, :].bitcast(BF16)

        s_x = [sem(f"s_xq{q}") for q in range(4)]
        s_rnnw = sem("s_rnnw")
        s_small = sem("s_small")
        s_w0 = sem("s_w0")
        s_wc = sem("s_wc")
        s_wf = sem("s_wf")
        s_out = sem("s_out")
        s_zero = sem("s_zero")
        s_id = sem("s_id")
        s_const = sem("s_const")
        s_condp = sem("s_condp")
        s_cond = sem("s_cond")
        s_xp = sem("s_xp")
        s_xt = sem("s_xt")
        s_rowp = sem("s_rowp")
        s_cols = sem("s_cols")
        s_silue = sem("s_silue")
        s_silu = sem("s_silu")
        s_modp = sem("s_modp")
        s_mod = sem("s_mod")
        s_be2 = sem("s_be2")
        s_step = sem("s_step")
        s_h = sem("s_h")
        s_inhi = sem("s_inhi")
        s_inlo = sem("s_inlo")
        s_res = sem("s_res")
        s_lgp = sem("s_lgp")
        s_lg = sem("s_lg")
        s_shift = sem("s_shift")
        s_ex = sem("s_ex")
        s_g3 = sem("s_g3")
        s_gTp = sem("s_gTp")
        s_gT = sem("s_gT")
        s_v = sem("s_v")
        s_w1hi0 = sem("s_w1hi0")
        s_w1lo0 = sem("s_w1lo0")
        s_w2hi0 = sem("s_w2hi0")
        s_w2lo0 = sem("s_w2lo0")
        s_z0 = sem("s_z0")
        s_g0 = sem("s_g0")
        s_hid0 = sem("s_hid0")
        s_hg0 = sem("s_hg0")
        s_hi0 = sem("s_hi0")
        s_lo0 = sem("s_lo0")
        s_y0 = sem("s_y0")
        s_x1 = sem("s_x1")
        s_x1hi = sem("s_x1hi")
        s_x1lo = sem("s_x1lo")
        s_b0 = sem("s_b0")
        s_b = sem("s_b")
        s_wv = sem("s_wv")
        s_wp = sem("s_wp")
        s_full = sem("s_full")
        s_hid = sem("s_hid")
        s_free = sem("s_free")
        s_lo = sem("s_lo")
        s_y = sem("s_y")
        s_yg = sem("s_yg")
        s_acc = sem("s_acc")
        s_agg = sem("s_agg")
        s_c = sem("s_c")
        s_chi = sem("s_chi")
        s_clo = sem("s_clo")
        s_fin = sem("s_fin")
        s_outp = sem("s_outp")
        s_nat = sem("s_nat")

        SLOTS_C = len(FIRST_C) + (NC_ - 1) * len(USUAL)
        ITEMS_C = NC_ * 2 * FC
        N_ITEMS0 = N0 * J0
        GC = h_f

        block = ctx.enter_context(nc.Block())
        x_v = x.rearrange("b (i s) d -> s b i d", s=2)
        out_v = out.rearrange("b (i s) d -> s b i d", s=2)

        def slot_base(phase, e):
            if phase == "c":
                return e * len(USUAL)
            if isinstance(e, int) and e == 0:
                return SLOTS_C
            return e * len(USUAL) + (SLOTS_C + len(FIRST_F) - len(USUAL))

        def item_base(phase, e):
            return e * (2 * FC) + (0 if phase == "c" else ITEMS_C)

        def yg_base(phase, e):
            return e * 2 + (0 if phase == "c" else 2 * NC_)

        def slots_of(phase, first):
            return (FIRST_C if phase == "c" else FIRST_F) if first else USUAL

        def experts(eng, count, body):
            body(0, True, False)
            with eng.Fori(1, count - 1) as e:
                body(e, False, False)
            body(count - 1, False, True)

        def acc_base(phase, e):
            return e * 2 + (0 if phase == "c" else 2 * (NC_ - 1))

        @block.sync
        def _(sp):
            def quarter(q):
                for s in range(2):
                    sp.dma_start(nat[64 * s:64 * s + 64, 4 * q:4 * q + 4, :],
                                 x_v[s, :, 4 * q:4 * q + 4, :]).then_inc(s_x[q], 16)
            sp.dma_start(cond_n[:], cond).then_inc(s_rnnw, 16)
            quarter(0)
            sp.dma_start(wh[:], Wh).then_inc(s_rnnw, 16)
            for q in range(1, 4):
                quarter(q)
            for dst, routed, shared in ((raw1, We1, ws1), (raw2, We2, ws2)):
                d = dst[:].rearrange("p (e f) -> p e f", f=D)
                sp.dma_start(d[:, 0:E0, :], routed.rearrange("e k f -> k e f")).then_inc(s_w0, 16)
                sp.dma_start(d[:, E0, :], shared).then_inc(s_w0, 16)
            d = rawc1[:].rearrange("p (e f) -> p e f", e=NC_)
            sp.dma_start(d[:, 0, :], sw1).then_inc(s_wc, 16)
            sp.dma_start(d[:, 1:NC_, :], ew1.rearrange("e k f -> k e f")).then_inc(s_wc, 16)
            d = rawc2[:].rearrange("p (e c f) -> p e c f", e=NC_, c=FC)
            sp.dma_start(d[:, 0, :, :], sw2.rearrange("(c p) f -> p c f", p=P)).then_inc(s_wc, 16)
            for e in range(EC):
                sp.dma_start(d[:, 1 + e, :, :], ew2[e].rearrange("(c p) f -> p c f", p=P)).then_inc(s_wc, 16)
            sp.wait_ge(s_w1lo0, N0)
            sp.wait_ge(s_w2lo0, N0)
            sp.dma_start(raw1[:].rearrange("p (e f) -> p e f", e=EF),
                         fw1.rearrange("e k f -> k e f")).then_inc(s_wf, 16)
            d = raw2[:].rearrange("p (e c f) -> p e c f", e=EF, c=FC)
            for e in range(EF):
                sp.dma_start(d[:, e, :, :], fw2[e].rearrange("(c p) f -> p c f", p=P)).then_inc(s_wf, 16)
            for j in range(J1):
                sp.wait_ge(s_nat, j + 1)
                for s in range(2):
                    sp.dma_start(out_v[s, :, 8 * j:8 * j + 8, :],
                                 nat[64 * s:64 * s + 64, 8 * j:8 * j + 8, :]).then_inc(s_out, 16)
            sp.wait_ge(s_out, 16 * 2 * J1)

        @block.gpsimd
        def _(pool):
            nc.gpsimd.memset(ident[:], 0.0).then_inc(s_zero, 1)
            pool.wait_ge(s_zero, 1)
            nc.gpsimd.affine_select(out=ident[:], in_=ident[:], compare_op=ALU.not_equal, fill=1.0, base=0,
                                    pattern=[[-1, P]], channel_multiplier=1).then_inc(s_id, 1)
            small = [(rows[R_B0:R_B0 + E0, :], Be1), (rows[R_B0 + E0:R_BC, :], bs1.unsqueeze(0)),
                     (rows[R_BC:R_BC + FC, :], sb1.rearrange("(c p) -> c p", p=P)),
                     (rows[R_BC + FC:R_BF, :], eb1.rearrange("e (c p) -> (e c) p", p=P)),
                     (rows[R_BF:R_YC, :], fb1.rearrange("e (c p) -> (e c) p", p=P)),
                     (rows[R_YC:R_YC + 1, :], sb2.unsqueeze(0)), (rows[R_YC + 1:R_YF, :], eb2),
                     (rows[R_YF:R_GF, :], fb2), (rows[R_GF:ROWS, :], fgw),
                     (wr[:], Wr), (br_b[:], br.partition_broadcast(P)),
                     (ctw_s[:], ctw), (ctb_b[:], ctb.partition_broadcast(P)),
                     (cgw_s[:], cgw.rearrange("(k p) e -> p k e", p=P)), (cgb_b[:], cgb.partition_broadcast(P))]
            for k in range(3):
                small += [(be2[GW * k:GW * k + E0, :], Be2), (be2[GW * k + E0:GW * k + N0, :], bs2.unsqueeze(0))]
            assert len(small) == N_SMALL
            for dst, src in small:
                pool.dma_start(dst, src).then_inc(s_small, 16)
            for tab in (lg0, take8, lgc, lgf, take8c, take8f):
                nc.gpsimd.memset(tab[:], NEG).then_inc(s_const, 1)
            nc.gpsimd.memset(gates[:], 0.0).then_inc(s_const, 1)
            nc.gpsimd.memset(ident_b[:], 0.0).then_inc(s_zero, 1)
            nc.gpsimd.memset(pick[:], 0.0).then_inc(s_zero, 1)
            pool.wait_ge(s_zero, 3)
            nc.gpsimd.affine_select(out=ident_b[:], in_=ident_b[:], compare_op=ALU.not_equal, fill=1.0, base=0,
                                    pattern=[[-1, P]], channel_multiplier=1).then_inc(s_id, 1)
            for k in range(3):
                nc.gpsimd.affine_select(out=pick[:], in_=pick[:], compare_op=ALU.not_equal, fill=1.0,
                                        base=-GW * k, pattern=[[-1, GW], [0, P]],
                                        channel_multiplier=1).then_inc(s_zero, 1)
                pool.wait_ge(s_zero, 4 + k)
            pool.wait_ge(s_const, 7)
            nc.gpsimd.memset(gates[:, :, E0:N0], 1.0).then_inc(s_const, 1)
            nc.gpsimd.memset(c_f[:], 0.0).then_inc(s_const, 1)

            for q in range(4):
                cut = slice(q * C0, (q + 1) * C0)
                pool.wait_ge(s_inhi, q + 1)
                nc.gpsimd.tensor_tensor(in_lo[:, cut], h_f[:, cut], in_hi[:, cut].bitcast(F32),
                                        ALU.subtract).then_inc(s_inlo, 1)

            def lo0(e, par, which):
                raw, hi, lo, s_hi, s_lo = ((raw1, w1h0, w1l0, s_w1hi0, s_w1lo0),
                                           (raw2, w2h0, w2l0, s_w2hi0, s_w2lo0))[which]
                pool.wait_ge(s_hi, e + 1)
                nc.gpsimd.tensor_tensor(lo[:, par, :], raw[:, bass.ds(e * D, D)], hi[:, par, :].bitcast(F32),
                                        ALU.subtract).then_inc(s_lo, 1)
            lo0(0, 0, 0)
            lo0(0, 0, 1)
            lo0(1, 1, 0)
            for q in range(4):
                cut = slice(q * C0, (q + 1) * C0)
                pool.wait_ge(s_h, T)
                nc.gpsimd.tensor_tensor(x_f[:, cut], x_f[:, cut], h_f[:, cut], ALU.add).then_inc(s_res, 1)
                if q == 0:
                    lo0(1, 1, 1)
            with pool.Fori(1, N0 // 2) as i:
                lo0(i * 2, 0, 0)
                lo0(i * 2, 0, 1)
                lo0(i * 2 + 1, 1, 0)
                lo0(i * 2 + 1, 1, 1)

            def w_lo(half, e, raws, count):
                hi, lo, raw = ((w1h, w1l, raws[0]), (w2h, w2l, raws[1]))[half // 2]
                at = half % 2 * 2 * P
                pool.wait_ge(s_wv, count)
                nc.gpsimd.tensor_tensor(lo[:, at:at + 2 * P], raw[:, bass.ds(e * (FC * P) + at, 2 * P)],
                                        hi[:, at:at + 2 * P].bitcast(F32), ALU.subtract).then_inc(s_wp, 1)

            def add(phase, e, j):
                acc = c_f if phase == "c" else x_f
                cut = slice(j * C1, (j + 1) * C1)
                pool.wait_ge(s_yg, yg_base(phase, e) + j + 1)
                nc.gpsimd.tensor_tensor(acc[:, cut], acc[:, cut], yg[:, j, :], ALU.add).then_inc(s_acc, 1)

            for half in range(4):
                w_lo(half, 0, (rawc1, rawc2), half + 1)

            def body(phase):
                raws = (rawc1, rawc2) if phase == "c" else (raw1, raw2)
                wbase = 0 if phase == "c" else 4 * NC_

                def one(e, first, last):
                    late = phase == "f" and first
                    if not last and not late:
                        add(phase, e, 0)
                    if not last or phase == "c":
                        nxt, src = (0, (raw1, raw2)) if last else (e + 1, raws)
                        for half in range(4):
                            w_lo(half, nxt, src, e * 4 + (wbase + 4 + half + 1))
                            if half == 2 and late:
                                add(phase, e, 0)
                    if not last:
                        add(phase, e, 1)
                return one
            experts(pool, NC_, body("c"))
            experts(pool, EF, body("f"))

        @block.scalar
        def _(act):
            act.dma_start(wx[:], Wx).then_inc(s_rnnw, 16)
            act.dma_start(rb_c[:], rb.unsqueeze(1)).then_inc(s_rnnw, 16)
            act.wait_ge(s_cond, 2)
            nc.scalar.activation(silu_e[:], cond2[:], ACT.Exp, scale=-1.0).then_inc(s_silue, 1)

            def route_exp(q, cut, n, shifts):
                act.wait_ge(s_shift, shifts)
                nc.scalar.activation(ex[:, cut, 0:n], g_r1[:, cut, 0:n], ACT.Exp).then_inc(s_ex, 1)

            act.wait_ge(s_rnnw, 64)
            for t in range(T):
                act.wait_ge(s_step, t + 1)
                nc.scalar.activation(h_f[:, t * B:(t + 1) * B], ps[:, t % 2, 0:B], ACT.Tanh,
                                     bias=rb_c[:, 0:1]).then_inc(s_h, 1)
                if t % 8 == 5 and t > 8:
                    q = t // 8 - 1
                    route_exp(q, slice(4 * q, 4 * q + 4), E0, q + 1)

            def w_hi0(par, cut, which):
                raw, hi, s = ((raw1, w1h0, s_w1hi0), (raw2, w2h0, s_w2hi0))[which]
                act.wait_ge(s_w0, 64)
                nc.scalar.activation(hi[:, par, :], raw[:, cut], ACT.Copy).then_inc(s, 1)
            w_hi0(0, slice(0, D), 0)
            w_hi0(0, slice(0, D), 1)
            route_exp(3, slice(12, 16), E0, 4)

            def item0(n, i, m, last):
                e_par, j = m // J0, m % J0
                act.wait_ge(s_z0, n + 1)
                if not (isinstance(n, int) and n < 2):
                    act.wait_ge(s_hg0, n - 1)
                e = i * 2 + e_par
                if j == 0:
                    act.wait_ge(s_b0, e + 1)
                nc.scalar.activation(hid[:, m % 2, 0:C0], bank(4 + m % 2), ACT.Gelu,
                                     bias=bias0_cur[:, e_par:e_par + 1]).then_inc(s_hid0, 1)
                if not (isinstance(n, int) and n == 0):
                    hi0(n - 1, (m - 1) % 8)
                if j == 0 and not (isinstance(n, int) and n == 0):
                    w_hi0(e_par, bass.ds(e * D, D), 1)
                if j == 0 and not (last and e_par == 1):
                    w_hi0(1 - e_par, bass.ds(e * D + D, D), 0)

            def hi0(n, m):
                act.wait_ge(s_hg0, n + 1)
                if not (isinstance(n, int) and n < 4):
                    act.wait_ge(s_y0, n - 3)
                nc.scalar.activation(hid_hi[:, m % 4, 0:C0], hid_g[:, m % 2, :], ACT.Copy).then_inc(s_hi0, 1)

            def pair0(i, first, last):
                for m in range(2 * J0):
                    item0(i * (2 * J0) + m, i, m, last)
            experts(act, N0 // 2, pair0)
            hi0(N_ITEMS0 - 1, 2 * J0 - 1)

            for q in range(4):
                cut = slice(q * C0, (q + 1) * C0)
                act.wait_ge(s_x1, q + 1)
                nc.scalar.activation(in_hi[:, cut], x_f[:, cut], ACT.Copy).then_inc(s_x1hi, 1)

            def c_hi(j):
                cut = slice(j * C1, (j + 1) * C1)
                act.wait_ge(s_c, j + 1)
                nc.scalar.activation(in_hi[:, cut], c_f[:, cut], ACT.Copy).then_inc(s_chi, 1)

            def body(phase):
                func = ACT.Gelu_apprx_tanh if phase == "c" else ACT.Relu

                def one(e, first, last):
                    n = 0
                    for k, (kind, j, f) in enumerate(slots_of(phase, first)):
                        S = slot_base(phase, e) + k
                        src = pair(4 + 2 * (k % 2))
                        act.wait_ge(s_full, S + 1)
                        if kind == "F":
                            item = item_base(phase, e) + n
                            bias = bias_cur[:, f:f + 1]
                            if j == 0 and f in (0, 2):
                                act.wait_ge(s_b, (e * 2 + (f // 2 + 1)) + (0 if phase == "c" else 2 * NC_))
                            if not (phase == "c" and first and n < 2):
                                act.wait_ge(s_lo, item - 1)
                            nc.scalar.activation(hid[:, n % 2, :], src, func, bias=bias).then_inc(s_hid, 1)
                            if not (phase == "c" and first and n < 4):
                                act.wait_ge(s_y, item - 3)
                            nc.scalar.activation(hid_hi[:, n % 4, :], src, func, bias=bias).then_inc(s_free, 1)
                            n += 1
                        elif kind == "G":
                            act.wait_ge(s_yg, yg_base(phase, e) + (j - 1))
                            nc.scalar.activation(GC[:, j * C1:(j + 1) * C1], src, ACT.Copy).then_inc(s_free, 1)
                        elif kind == "A":
                            nc.scalar.activation(la[:], src[:, 0:EC], ACT.Copy).then_inc(s_free, 1)
                        elif kind == "R":
                            nc.scalar.activation(lgf[:, :, 0:EF],
                                                 src[:, 0:TILES * EF].rearrange("p (i e) -> p i e", e=EF),
                                                 ACT.Copy).then_inc(s_free, 1)
                        else:
                            nc.scalar.activation(gates_T[:], src[0:3 * GW, :].bitcast(BF16), ACT.Copy).then_inc(s_free, 1)
                        if phase == "c" and first and k == 6:
                            act.wait_ge(s_shift, 5)
                            nc.scalar.activation(ex[:, 0:1, 0:EC], g_r1[:, 0:1, 0:EC], ACT.Exp).then_inc(s_ex, 1)
                        if phase == "c" and last and k == 6:
                            c_hi(0)
                        if phase == "f" and first and k == 0:
                            c_hi(1)
                        if phase == "f" and first and k == 6:
                            act.wait_ge(s_shift, 6)
                            nc.scalar.activation(ex[:, :, 0:EF], g_r1[:, :, 0:EF], ACT.Exp).then_inc(s_ex, 1)
                return one
            experts(act, NC_, body("c"))
            experts(act, EF, body("f"))
            for j in range(J1):
                act.wait_ge(s_outp, j + 1)
                nc.scalar.activation(nat[:, 8 * j:8 * j + 8, :], pair(4 + 2 * j).rearrange("p (i d) -> p i d", d=D),
                                     ACT.Copy).then_inc(s_nat, 1)

        @block.vector
        def _(dve):
            chain = [0]

            def link(ins):
                chain[0] += 1
                ins.then_inc(s_v, 1)
                dve.wait_ge(s_v, chain[0])

            V = nc.vector
            dve.wait_ge(s_condp, 1)
            for k in range(2):
                V.tensor_copy(cond2[:, k, :], ps[:, 6, 0:B]).then_inc(s_cond, 1)
            for q in range(4):
                dve.wait_ge(s_xp, q + 1)
                V.tensor_copy(x_f[:, q * C0:(q + 1) * C0], bank(4 + q % 2)).then_inc(s_xt, 1)
            dve.wait_ge(s_rowp, 1)
            V.tensor_copy(cols[:], ps[:, 6, 128:128 + ROWS]).then_inc(s_cols, 1)
            dve.wait_ge(s_silue, 1)
            link(V.tensor_scalar(silu_e[:], silu_e[:], 1.0, None, ALU.add))
            link(V.reciprocal(silu_e[:], silu_e[:]))
            V.tensor_tensor(silu2[:], cond2[:], silu_e[:], ALU.mult).then_inc(s_silu, 1)
            dve.wait_ge(s_small, 16 * N_SMALL)
            dve.wait_ge(s_modp, 1)
            V.tensor_tensor(mod[:], ps[:, 6, 256:256 + 2 * EC], ctb_b[:], ALU.add).then_inc(s_mod, 1)
            dve.wait_ge(s_mod, 1)
            V.tensor_scalar(mod[:, 0:EC], mod[:, 0:EC], 1.0, None, ALU.add).then_inc(s_mod, 1)
            link(V.tensor_copy(be2_p[:, 0, :], be2[:]))
            link(V.tensor_tensor(be2_r1[:], be2[:], be2_p[:, 0, :], ALU.subtract))
            link(V.tensor_copy(be2_p[:, 1, :], be2_r1[:]))
            link(V.tensor_tensor(be2_r2[:], be2_r1[:], be2_p[:, 1, :], ALU.subtract))
            V.tensor_copy(be2_p[:, 2, :], be2_r2[:]).then_inc(s_be2, 1)

            def topk(lg, tiles, n, k, take, part, pad):
                if part == 0:
                    for i in tiles:
                        V.max(top8[:, i, :], lg[:, i, 0:max(n, 8)]).then_inc(s_v, 1)
                        chain[0] += 1
                    dve.wait_ge(s_v, chain[0])
                    cut = slice(tiles[0], tiles[-1] + 1)
                    link(V.tensor_copy(take[:, cut, 0:k], top8[:, cut, 0:k]))
                else:
                    for i in tiles:
                        V.match_replace(left[:, i, 0:pad], take[:, i, :], lg[:, i, 0:pad], TAKEN).then_inc(s_v, 1)
                        chain[0] += 1
                    dve.wait_ge(s_v, chain[0])

            def shift(lg, tiles, n):
                cut = slice(tiles[0], tiles[-1] + 1)
                link(V.tensor_tensor(taken[:, cut, 0:n], left[:, cut, 0:n], lg[:, cut, 0:n], ALU.not_equal))
                V.tensor_tensor(g_r1[:, cut, 0:n], lg[:, cut, 0:n],
                                top8[:, cut, 0:1].broadcast_to([P, len(tiles), n]),
                                ALU.subtract).then_inc(s_shift, 1)

            def softmax(tiles, n, exs, out_g):
                cut = slice(tiles[0], tiles[-1] + 1)
                dve.wait_ge(s_ex, exs)
                link(V.tensor_reduce(ssum[:, cut], ex[:, cut, 0:n], AX, ALU.add))
                link(V.reciprocal(rsum[:, cut], ssum[:, cut]))
                link(V.tensor_tensor(ex[:, cut, 0:n], ex[:, cut, 0:n], taken[:, cut, 0:n], ALU.mult))
                link(V.tensor_tensor(out_g, ex[:, cut, 0:n],
                                     rsum[:, cut].unsqueeze(2).broadcast_to([P, len(tiles), n]), ALU.mult))

            def split3(tiles, n):
                cut = slice(tiles[0], tiles[-1] + 1)
                part = [gates3[:, cut, GW * k:GW * k + n] for k in range(3)]
                link(V.tensor_copy(part[0], gates[:, cut, 0:n]))
                link(V.tensor_tensor(g_r1[:, cut, 0:n], gates[:, cut, 0:n], part[0], ALU.subtract))
                link(V.tensor_copy(part[1], g_r1[:, cut, 0:n]))
                link(V.tensor_tensor(g_r2[:, cut, 0:n], g_r1[:, cut, 0:n], part[1], ALU.subtract))
                V.tensor_copy(part[2], g_r2[:, cut, 0:n]).then_inc(s_g3, 1)

            def gates_T_out(q):
                dve.wait_ge(s_gTp, q + 1)
                V.tensor_copy(gates_T[:, q * C0:(q + 1) * C0],
                              GT_BANK[:, q % 2 * C0:(q % 2 + 1) * C0]).then_inc(s_gT, 1)

            dve.wait_ge(s_const, 8)
            for q in range(4):
                dve.wait_ge(s_h, 8 * q + 8)
                cut = slice(q * C0, (q + 1) * C0)
                V.tensor_copy(in_hi[:, cut], h_f[:, cut]).then_inc(s_inhi, 1)
                tiles = list(range(4 * q, 4 * q + 4))
                dve.wait_ge(s_lgp, q + 1)
                V.tensor_tensor(lg0[:, 4 * q:4 * q + 4, 0:E0],
                                ps[:, 7, 128 * q:128 * q + 128].rearrange("p (i e) -> p i e", e=GW)[:, :, 0:E0],
                                br_b[:].unsqueeze(1).broadcast_to([P, 4, E0]), ALU.add).then_inc(s_lg, 1)
                dve.wait_ge(s_lg, q + 1)
                topk(lg0, tiles, E0, K0, take8, 0, 0)
                topk(lg0, tiles, E0, K0, take8, 1, E0 + 9)
                shift(lg0, tiles, E0)
                softmax(tiles, E0, q + 1, gates[:, 4 * q:4 * q + 4, 0:E0])
                split3(tiles, GW)
                gates_T_out(q)

            def bias0(e, par):
                V.tensor_scalar(bias0_cur[:, par:par + 1], cols[:, bass.ds(e + R_B0, 1)], 0.0, None,
                                ALU.add).then_inc(s_b0, 1)

            def bias1(phase, e, half):
                at = e * FC + ((R_BC if phase == "c" else R_BF) + 2 * half)
                V.tensor_scalar(bias_cur[:, 2 * half:2 * half + 2], cols[:, bass.ds(at, 2)], 0.0, None,
                                ALU.add).then_inc(s_b, 1)

            def hg0(n, m):
                dve.wait_ge(s_hid0, n + 1)
                dve.wait_ge(s_g0, n + 1)
                if not (isinstance(n, int) and n < 2):
                    dve.wait_ge(s_lo0, n - 1)
                V.tensor_tensor(hid_g[:, m % 2, :], hid[:, m % 2, 0:C0], bank(6 + m % 2), ALU.mult).then_inc(s_hg0, 1)

            def lo0(n, m):
                dve.wait_ge(s_hi0, n + 1)
                V.tensor_tensor(hid_lo[:, m % 4, 0:C0], hid_g[:, m % 2, :], hid_hi[:, m % 4, 0:C0].bitcast(F32),
                                ALU.subtract).then_inc(s_lo0, 1)

            def pair0(i, first, last):
                for m in range(2 * J0):
                    n = i * (2 * J0) + m
                    hg0(n, m)
                    if not (first and m == 0):
                        lo0(n - 1, (m - 1) % 8)
                    if m % J0 == 0 and not (last and m == J0):
                        bias0(i * 2 + (m // J0 + 1), 1 - m // J0)
            bias0(0, 0)
            bias1("c", 0, 0)
            bias1("c", 0, 1)
            experts(dve, N0 // 2, pair0)
            lo0(N_ITEMS0 - 1, 2 * J0 - 1)

            def w_hi(half, e, raws):
                hi, raw = ((w1h, raws[0]), (w2h, raws[1]))[half // 2]
                at = half % 2 * 2 * P
                V.tensor_copy(hi[:, at:at + 2 * P], raw[:, bass.ds(e * (FC * P) + at, 2 * P)]).then_inc(s_wv, 1)

            dve.wait_ge(s_wc, 16 * N_WC)
            for half in range(4):
                w_hi(half, 0, (rawc1, rawc2))

            def x1_lo(q):
                cut = slice(q * C0, (q + 1) * C0)
                dve.wait_ge(s_x1hi, q + 1)
                V.tensor_tensor(in_lo[:, cut], x_f[:, cut], in_hi[:, cut].bitcast(F32), ALU.subtract).then_inc(s_x1lo, 1)
            for q in range(4):
                cut = slice(q * C0, (q + 1) * C0)
                dve.wait_ge(s_res, q + 1)
                dve.wait_ge(s_y0, N_ITEMS0 - J0 + q + 1)
                V.tensor_tensor(x_f[:, cut], x_f[:, cut], bank(q), ALU.add).then_inc(s_x1, 1)
                if q:
                    x1_lo(q - 1)
            x1_lo(3)

            def means(part):
                seg = x_f[:].rearrange("p (t b) -> p b t", b=B)
                cuts = (slice(0, T_HEAD), slice(T_HEAD, T_HEAD + T_WRIST), slice(T_HEAD + T_WRIST, T))
                if part < 3:
                    if part == 0:
                        dve.wait_ge(s_x1, 4)
                    V.tensor_reduce(agg_s[:, part, :], seg[:, :, cuts[part]], AX, ALU.add).then_inc(s_v, 1)
                    chain[0] += 1
                    return
                dve.wait_ge(s_v, chain[0])
                head, wrist, prop = (agg_s[:, k, :] for k in range(3))
                link(V.tensor_tensor(agg_t[:, 1, :], head, prop, ALU.add))
                link(V.tensor_tensor(agg_t[:, 2, :], wrist, prop, ALU.add))
                link(V.tensor_tensor(agg_t[:, 0, :], agg_t[:, 1, :], wrist, ALU.add))
                for k, count in enumerate((T, T - T_WRIST, T - T_HEAD)):
                    V.tensor_scalar(agg[:, k, :, :], agg_t[:, k, :].unsqueeze(1).broadcast_to([P, 2, B]),
                                    1.0 / count, None, ALU.mult).then_inc(s_agg, 1)

            def gate_c(part):
                if part == 0:
                    dve.wait_ge(s_free, 5)
                    dve.wait_ge(s_mod, 2)
                    link(V.tensor_tensor(la[:], la[:], cgb_b[:], ALU.add))
                    link(V.tensor_tensor(la[:], la[:], mod[:, 0:EC], ALU.mult))
                    link(V.tensor_tensor(lgc[:, 0, 0:EC], la[:], mod[:, EC:2 * EC], ALU.add))
                    topk(lgc, [0], EC, KC, take8c, 0, 0)
                    topk(lgc, [0], EC, KC, take8c, 1, 16)
                    shift(lgc, [0], EC)
                elif part == 1:
                    softmax([0], EC, 5, wbe[:].unsqueeze(1))
                    link(V.tensor_reduce(wsum[:], wbe[:], AX, ALU.add))
                    link(V.tensor_scalar(wsum[:], wsum[:], 1e-8, None, ALU.add))
                    link(V.reciprocal(wrec[:], wsum[:]))
                    link(V.tensor_scalar(wbe[:], wbe[:], wrec[:, 0:1], None, ALU.mult))
                    link(V.tensor_copy(gates[:, :, 1:NC_], wbe[:].unsqueeze(1).broadcast_to([P, TILES, EC])))
                    link(V.memset(gates[:, T_HEAD // 2:(T_HEAD + T_WRIST) // 2, 2:3], 0.0))
                    link(V.memset(gates[:, 0:T_HEAD // 2, 3:4], 0.0))
                else:
                    split3(list(range(TILES)), NC_)

            def route_f(part):
                tiles = list(range(TILES))
                if part == 0:
                    dve.wait_ge(s_free, SLOTS_C + 3)
                    topk(lgf, tiles, EF, KF, take8f, 0, 0)
                elif part == 1:
                    topk(lgf, tiles, EF, KF, take8f, 1, 16)
                elif part == 2:
                    shift(lgf, tiles, EF)
                else:
                    softmax(tiles, EF, 6, gates[:, :, 0:EF])
                    split3(tiles, EF)

            def evac(phase, e, j, gated, slot):
                row = (R_YC if phase == "c" else R_YF) + 0
                bias = cols[:, bass.ds(e + row, 1)]
                dve.wait_ge(s_y, item_base(phase, e) + (4 * j + 4))
                if not gated:
                    V.tensor_scalar(yg[:, j, :], pair(2 * j), bias, None, ALU.add).then_inc(s_yg, 1)
                    return
                dve.wait_ge(s_free, slot + 1)
                if phase == "f" and isinstance(e, int) and e == 0:
                    dve.wait_ge(s_c, 2)
                else:
                    dve.wait_ge(s_acc, acc_base(phase, e) + (j - 1))
                V.scalar_tensor_tensor(yg[:, j, :], pair(2 * j), bias, GC[:, j * C1:(j + 1) * C1],
                                       ALU.add, ALU.mult).then_inc(s_yg, 1)

            def total(phase, j):
                count = NC_ if phase == "c" else EF
                acc, s = (c_f, s_c) if phase == "c" else (x_f, s_fin)
                cut = slice(j * C1, (j + 1) * C1)
                dve.wait_ge(s_yg, yg_base(phase, count - 1) + j + 1)
                dve.wait_ge(s_acc, acc_base(phase, count - 1) + (j - 1))
                V.tensor_tensor(acc[:, cut], acc[:, cut], yg[:, j, :], ALU.add).then_inc(s, 1)

            def c_lo(j):
                cut = slice(j * C1, (j + 1) * C1)
                dve.wait_ge(s_chi, j + 1)
                V.tensor_tensor(in_lo[:, cut], c_f[:, cut], in_hi[:, cut].bitcast(F32), ALU.subtract).then_inc(s_clo, 1)

            def body(phase):
                raws = (rawc1, rawc2) if phase == "c" else (raw1, raw2)

                def one(e, first, last):
                    slots = slots_of(phase, first)
                    base = slot_base(phase, e)
                    gslot = {j: base + k for k, (kind, j, _) in enumerate(slots) if kind == "G"}
                    late = phase == "f" and first
                    nxt, src = (0, (raw1, raw2)) if last else (e + 1, raws)
                    prefetch = not (last and phase == "f")
                    gated = not (phase == "c" and first)
                    n = 0
                    for k, (kind, j, f) in enumerate(slots):
                        if kind != "F":
                            continue
                        dve.wait_ge(s_free, base + (k + 1))
                        V.tensor_tensor(hid_lo[:, n % 4, :], hid[:, n % 2, :], hid_hi[:, n % 4, :].bitcast(F32),
                                        ALU.subtract).then_inc(s_lo, 1)
                        n += 1
                        if (j, f) == (0, 0) and late:
                            c_lo(1)
                        if phase == "c" and first:
                            if (j, f) == (0, 0):
                                means(0)
                                means(1)
                            if (j, f) == (0, 1):
                                means(2)
                                means(3)
                        if late and (j, f) in ((0, 2), (0, 3), (1, 0), (1, 1)):
                            route_f({(0, 2): 0, (0, 3): 1, (1, 0): 2, (1, 1): 3}[j, f])
                        if (j, f) == (1, 0):
                            if not late:
                                evac(phase, e, 0, gated, gslot.get(0))
                            if last:
                                total(phase, 0)
                            if phase == "c" and first:
                                gate_c(0)
                        if (j, f) == (1, 1):
                            if prefetch and last:
                                dve.wait_ge(s_wf, 16 * N_WF)
                            if prefetch:
                                w_hi(0, nxt, src)
                                bias1("f" if last else phase, nxt, 0)
                        if (j, f) == (1, 2):
                            if phase == "c" and last:
                                c_lo(0)
                            if phase == "c" and first:
                                gate_c(1)
                                gate_c(2)
                        if (j, f) == (1, 3) and prefetch:
                            w_hi(1, nxt, src)
                            bias1("f" if last else phase, nxt, 1)
                            dve.wait_ge(s_y, item_base(phase, e) + (4 + 2))
                            w_hi(2, nxt, src)
                    if late:
                        evac(phase, e, 0, gated, gslot.get(0))
                    evac(phase, e, 1, gated, gslot.get(1))
                    if last:
                        total(phase, 1)
                    if prefetch:
                        w_hi(3, nxt, src)
                return one
            experts(dve, NC_, body("c"))
            experts(dve, EF, body("f"))

        @block.tensor
        def _(pe):
            M = nc.tensor

            def pick_of(e):
                return pick[:].rearrange("p e m -> p (e m)")[:, bass.ds(e * P, P)]

            def mm3(o, wts, src, start=True, stop=True):
                (wa, wb), (va, vb) = wts, src
                M.matmul(o, wa, va, start=start, stop=False, skip_group_check=True)
                M.matmul(o, wa, vb, start=False, stop=False, skip_group_check=True)
                return M.matmul(o, wb, va, start=False, stop=stop, skip_group_check=True)

            def x_tiles(q):
                pe.wait_ge(s_x[q], 32)
                if q >= 2:
                    pe.wait_ge(s_xt, q - 1)
                for k in range(4):
                    last = M.transpose(ps[:, 4 + q % 2, k * P:(k + 1) * P], nat[:, 4 * q + k, :], ident[:])
                last.then_inc(s_xp, 1)

            pe.wait_ge(s_id, 1)
            pe.wait_ge(s_rnnw, 64)
            M.transpose(ps[:, 6, 0:B], cond_n[:], ident[0:B, 0:B]).then_inc(s_condp, 1)
            x_tiles(0)

            def x_part(t):
                if t % 8 == 0:
                    pe.wait_ge(s_xt, t // 8 + 1)
                M.matmul(ps[:, t % 2, 0:B], wx[:], x_f[:, t * B:(t + 1) * B], start=True, stop=False)

            def logits(q):
                if q:
                    pe.wait_ge(s_lg, q)
                else:
                    pe.wait_ge(s_small, 16 * N_SMALL)
                for i in range(4 * q, 4 * q + 4):
                    last = M.matmul(ps[:, 7, i * GW:i * GW + E0], h_f[:, i * P:(i + 1) * P], wr[:], start=True, stop=True)
                last.then_inc(s_lgp, 1)

            def gates_turn(q):
                pe.wait_ge(s_g3, q + 1)
                if q == 0:
                    pe.wait_ge(s_id, 2)
                    pe.wait_ge(s_mod, 1)
                if q >= 2:
                    pe.wait_ge(s_gT, q - 1)
                for k in range(4):
                    at = q % 2 * C0 + k * P
                    last = M.transpose(GT_BANK[:, at:at + P], gates3[:, 4 * q + k, :], ident_b[:])
                last.then_inc(s_gTp, 1)

            x_part(0)
            for t in range(T):
                if t == 0:
                    pe.wait_ge(s_cond, 2)
                    prev = cond2[:, 0, :]
                else:
                    pe.wait_ge(s_h, t)
                    prev = h_f[:, (t - 1) * B:t * B]
                M.matmul(ps[:, t % 2, 0:B], wh[:], prev, start=False, stop=True).then_inc(s_step, 1)
                if t + 1 < T:
                    x_part(t + 1)
                if t in (1, 2, 3):
                    x_tiles(t)
                if t == 7:
                    pe.wait_ge(s_small, 16 * N_SMALL)
                    M.transpose(ps[:, 6, 128:128 + ROWS], rows[:], ident[0:ROWS, 0:ROWS]).then_inc(s_rowp, 1)
                if t == 8:
                    pe.wait_ge(s_silu, 1)
                    M.matmul(ps[:, 6, 256:256 + 2 * EC], silu2[:].rearrange("p a b -> p (a b)"), ctw_s[:],
                             start=True, stop=True).then_inc(s_modp, 1)
                if t % 8 == 0 and t:
                    logits(t // 8 - 1)
                if t % 8 == 7 and t > 8:
                    gates_turn(t // 8 - 1)
            pe.wait_ge(s_h, T)
            logits(3)

            def item0(n, i, m, first):
                e_par, j = m // J0, m % J0
                cut = slice(j * C0, (j + 1) * C0)
                e = i * 2 + e_par
                if j == 0:
                    pe.wait_ge(s_w1lo0, e + 1)
                if first and e_par == 0:
                    pe.wait_ge(s_inlo, j + 1)
                if not (first and m < 2):
                    pe.wait_ge(s_hid0, n - 1)
                mm3(bank(4 + m % 2), (w1h0[:, e_par, :], w1l0[:, e_par, :]),
                    (in_hi[:, cut], in_lo[:, cut])).then_inc(s_z0, 1)
                if first and m == 0:
                    gates_turn(3)
                    pe.wait_ge(s_gT, 4)
                if not (first and m < 2):
                    pe.wait_ge(s_hg0, n - 1)
                sel = pick_of(e)
                M.matmul(bank(6 + m % 2), sel, gates_T[:, cut], start=True, stop=True).then_inc(s_g0, 1)

            def second0(n, m, first, last):
                e_par, j = m // J0, m % J0
                cut = slice(j * C0, (j + 1) * C0)
                if first and e_par == 0:
                    pe.wait_ge(s_be2, 1)
                    for k in range(3):
                        M.matmul(bank(j), be2_p[:, k, :], gates_T[:, cut], start=k == 0, stop=False,
                                 skip_group_check=True)
                pe.wait_ge(s_lo0, n + 1)
                mm3(bank(j), (w2h0[:, e_par, :], w2l0[:, e_par, :]),
                    (hid_hi[:, m % 4, 0:C0], hid_lo[:, m % 4, 0:C0]),
                    start=False, stop=last and e_par == 1).then_inc(s_y0, 1)

            def pair0(i, first, last):
                for m in range(2 * J0):
                    item0(i * (2 * J0) + m, i, m, first)
                    if not (first and m < LAG0):
                        b = m - LAG0
                        w = b % (2 * J0)
                        if w % J0 == 0:
                            pe.wait_ge(s_w2lo0, i * 2 + (w // J0 + 1))
                        second0(i * (2 * J0) + b, w, first and b >= 0, last and b >= 0)
            pe.wait_ge(s_zero, 6)
            experts(pe, N0 // 2, pair0)
            for n in range(N_ITEMS0 - LAG0, N_ITEMS0):
                second0(n, n % (2 * J0), False, True)

            def second(phase, e, n, j, f):
                item = item_base(phase, e) + n
                wbase = 0 if phase == "c" else 4 * NC_
                if j == 0 and f in (0, 2):
                    pe.wait_ge(s_wp, e * 4 + (wbase + 3 + f // 2))
                if f == 0 and not (phase == "c" and isinstance(e, int) and e == 0):
                    pe.wait_ge(s_yg, yg_base(phase, e) + (j - 1))
                pe.wait_ge(s_lo, item + 1)
                cut = slice(f * P, (f + 1) * P)
                for h in range(2):
                    s = slice(h * 512, h * 512 + 512)
                    last = mm3(bank(2 * j + h), (w2h[:, cut], w2l[:, cut]),
                               (hid_hi[:, n % 4, s], hid_lo[:, n % 4, s]), start=f == 0, stop=f == FC - 1)
                last.then_inc(s_y, 1)

            def body(phase):
                def one(e, first, last):
                    slots = slots_of(phase, first)
                    wbase = 0 if phase == "c" else 4 * NC_
                    items = {k: sum(s[0] == "F" for s in slots[:k]) for k in range(len(slots))}
                    for k, (kind, j, f) in enumerate(slots):
                        S = slot_base(phase, e) + k
                        b0 = 4 + 2 * (k % 2)
                        if not (phase == "c" and first and k < 2):
                            pe.wait_ge(s_free, S - 1)
                        if kind == "F":
                            if j == 0 and f in (0, 2):
                                pe.wait_ge(s_wp, e * 4 + (wbase + 1 + f // 2))
                            if first and f == 0:
                                if phase == "c":
                                    pe.wait_ge(s_x1lo, 2 * j + 2)
                                else:
                                    pe.wait_ge(s_clo, j + 1)
                            cut = slice(f * P, (f + 1) * P)
                            for h in range(2):
                                s = slice(j * C1 + h * 512, j * C1 + h * 512 + 512)
                                op = mm3(bank(b0 + h), (w1h[:, cut], w1l[:, cut]), (in_hi[:, s], in_lo[:, s]))
                        elif kind == "G":
                            sel = pick_of(e)
                            for h in range(2):
                                s = slice(j * C1 + h * 512, j * C1 + h * 512 + 512)
                                if first:
                                    pe.wait_ge(s_free, S - k + 9)
                                op = M.matmul(bank(b0 + h), sel, gates_T[:, s], start=True, stop=True)
                        elif kind == "A":
                            pe.wait_ge(s_agg, 3)
                            for q in range(3):
                                op = M.matmul(ps[:, b0, 0:EC], agg[:, q, :, :].rearrange("p a b -> p (a b)"),
                                              cgw_s[:, q, :], start=q == 0, stop=q == 2)
                        elif kind == "R":
                            pe.wait_ge(s_c, 2)
                            for i in range(TILES):
                                op = M.matmul(ps[:, b0, i * EF:(i + 1) * EF], c_f[:, i * P:(i + 1) * P],
                                              cols[:, R_GF:R_GF + EF], start=True, stop=True)
                        else:
                            pe.wait_ge(s_g3, 5 if phase == "c" else 6)
                            turned = pair(b0)[0:3 * GW, :].bitcast(BF16)
                            for i in range(TILES):
                                op = M.transpose(turned[:, i * P:(i + 1) * P], gates3[:, i, :], ident_b[:])
                        op.then_inc(s_full, 1)
                        if k >= LAG1:
                            if slots[k - LAG1][0] == "F":
                                second(phase, e, items[k - LAG1], *slots[k - LAG1][1:])
                        elif not (phase == "c" and first):
                            kind, j, f = USUAL[k - LAG1]
                            if kind == "F":
                                where = ("c", NC_ - 1) if first else (phase, e - 1)
                                second(*where, 2 * FC - 1, j, f)
                return one
            experts(pe, NC_, body("c"))
            experts(pe, EF, body("f"))

            second("f", EF - 1, 2 * FC - 1, 1, FC - 1)

            pe.wait_ge(s_free, slot_base("f", EF))
            for j in range(J1):
                pe.wait_ge(s_fin, j + 1)
                for i in range(8):
                    op = M.transpose(ps[:, 4 + 2 * j + i // 4, (i % 4) * P:(i % 4 + 1) * P],
                                     x_f[:, (8 * j + i) * P:(8 * j + i + 1) * P], ident[:])
                op.then_inc(s_outp, 1)


_INS = ['x', 'cond_1024', 'L0_cond_Wx', 'L0_cond_Wh', 'L0_cond_b', 'L0_ffn_ws1', 'L0_ffn_bs1', 'L0_ffn_ws2',
        'L0_ffn_bs2', 'L0_ffn_We1', 'L0_ffn_Be1', 'L0_ffn_We2', 'L0_ffn_Be2', 'L0_ffn_Wr', 'L0_ffn_br',
        'L1_cond_gate_w', 'L1_cond_gate_b', 'L1_cond_time_w', 'L1_cond_time_b', 'L1_cond_ew1', 'L1_cond_eb1',
        'L1_cond_ew2', 'L1_cond_eb2', 'L1_cond_sw1', 'L1_cond_sb1', 'L1_cond_sw2', 'L1_cond_sb2',
        'L1_ffn_gate_w', 'L1_ffn_w1', 'L1_ffn_b1', 'L1_ffn_w2', 'L1_ffn_b2']


def kernel(**inputs):
    import numpy as _np
    import concourse.bacc as _bacc
    from concourse import mybir as _mybir
    from concourse.bass_utils import run_bass_kernel_spmd as _run

    nc = _bacc.Bacc("TRN2", target_bir_lowering=False, num_devices=1)
    arrays, args = {}, []
    for name in _INS:
        a = _np.ascontiguousarray(inputs[name])
        arrays[f"in_{name}_dram"] = a
        args.append(nc.dram_tensor(f"in_{name}_dram", a.shape, _mybir.dt.from_np(a.dtype), kind="ExternalInput").ap())
    args.append(nc.dram_tensor("out_0_dram", (B, T, D), F32, kind="ExternalOutput").ap())
    build(nc, *args)
    r = _run(nc, [arrays], core_ids=[0])
    return r.results[0]["out_0_dram"]
```

```python
from contextlib import ExitStack

import concourse.bass as bass
from concourse import mybir

ACT = mybir.ActivationFunctionType
ALU = mybir.AluOpType
AX = mybir.AxisListType.X
F32 = mybir.dt.float32
F32R = mybir.dt.float32r
BF16 = mybir.dt.bfloat16

B, T, D = 64, 32, 128
NT = B * T
P = 128
TILES = NT // P
C0 = 512
J0 = NT // C0
C1 = 1024
J1 = NT // C1
E0, K0 = 31, 3
N0 = E0 + 1
EC, KC = 4, 2
NC_ = EC + 1
EF, KF = 8, 2
FC = 4
GW = 32
T_HEAD = T_WRIST = T // 3
NEG = -3.0e38
TAKEN = 3.0e38

R_B0 = 0
R_BC = R_B0 + N0
R_BF = R_BC + NC_ * FC
R_YC = R_BF + EF * FC
R_YF = R_YC + NC_
R_GF = R_YF + EF
ROWS = R_GF + EF

F0, F1 = ([("F", j, f) for f in range(FC)] for j in range(2))
SLOTS = {("c", True): F0 + [("A", 0, 0)] + F1 + [("X", 0, 0)],
         ("c", False): F0 + F1,
         ("f", True): F0[:2] + [("R", 0, 0)] + F0[2:] + F1[:3] + [("X", 0, 0), ("G", 0, 0)] + F1[3:] + [("G", 1, 0)],
         ("f", False): F0 + [("G", 0, 0)] + F1 + [("G", 1, 0)]}
ALL = ((0, C1), (0, C1))
SEES = [ALL, ALL, ((0, T_HEAD * B), ((T_HEAD + T_WRIST) * B - C1, C1)), ((T_HEAD * B, C1), (0, C1)), ALL]
LAG0 = 3
N_SMALL = 15
N_WC = 3 + EC
N_WF = 1 + EF
LAG1 = 2


def build(nc, x, cond, Wx, Wh, rb, ws1, bs1, ws2, bs2, We1, Be1, We2, Be2, Wr, br,
          cgw, cgb, ctw, ctb, ew1, eb1, ew2, eb2, sw1, sb1, sw2, sb2, fgw, fw1, fb1, fw2, fb2, out):
    ctx = ExitStack()
    with ctx:
        def sb(name, shape, dt):
            return ctx.enter_context(nc.sbuf_tensor(name, shape, dt))

        def sem(name):
            return ctx.enter_context(nc.semaphore(name))

        nat = sb("nat", [P, TILES, D], F32)
        c_f = sb("c_f", [P, NT], F32)
        x_f = sb("x_f", [P, NT], F32)
        h_f = sb("h_f", [P, NT], F32)
        in_hi = sb("in_hi", [P, NT], F32R)
        in_lo = sb("in_lo", [P, NT], F32R)
        raw1 = sb("raw1", [P, N0 * D], F32)
        raw2 = sb("raw2", [P, N0 * D], F32)
        rawc1 = sb("rawc1", [P, NC_ * FC * P], F32)
        rawc2 = sb("rawc2", [P, NC_ * FC * P], F32)
        w1h0 = sb("w1h0", [P, 2, D], F32R)
        w1l0 = sb("w1l0", [P, 2, D], F32R)
        w2h0 = sb("w2h0", [P, 2, D], F32R)
        w2l0 = sb("w2l0", [P, 2, D], F32R)
        w1h = sb("w1h", [P, FC * P], F32R)
        w1l = sb("w1l", [P, FC * P], F32R)
        w2h = sb("w2h", [P, FC * P], F32R)
        w2l = sb("w2l", [P, FC * P], F32R)
        hid = sb("hid", [P, 2, C1], F32)
        hid_hi = sb("hid_hi", [P, 4, C1], F32R)
        hid_lo = sb("hid_lo", [P, 4, C1], F32R)
        yg = sb("yg", [P, 2, C1], F32)
        gates_T = sb("gates_T", [3 * GW, NT], BF16)
        gates3 = sb("gates3", [P, TILES, 3 * GW], BF16)
        gc_w = sb("gc_w", [B, EC, P], F32)
        gc_T = sb("gc_T", [P, EC, B], F32)
        gates = sb("gates", [P, TILES, GW], F32)
        g_r1 = sb("g_r1", [P, TILES, GW], F32)
        g_r2 = sb("g_r2", [P, TILES, GW], F32)
        pick = sb("pick", [3 * GW, GW, P], BF16)
        ident = sb("ident", [P, P], F32)
        ident_b = sb("ident_b", [P, P], BF16)
        lg0 = sb("lg0", [P, TILES, E0 + 9], F32)
        lgc = sb("lgc", [P, 1, 16], F32)
        lgf = sb("lgf", [P, TILES, 16], F32)
        left = sb("left", [P, TILES, E0 + 9], F32)
        top8 = sb("top8", [P, TILES, 8], F32)
        take8 = sb("take8", [P, TILES, 8], F32)
        take8c = sb("take8c", [P, 1, 8], F32)
        take8f = sb("take8f", [P, TILES, 8], F32)
        ex = sb("ex", [P, TILES, GW], F32)
        taken = sb("taken", [P, TILES, GW], F32)
        ssum = sb("ssum", [P, TILES], F32)
        rsum = sb("rsum", [P, TILES], F32)
        cond_n = sb("cond_n", [B, D], F32)
        cond2 = sb("cond2", [P, 2, B], F32)
        silu_e = sb("silu_e", [P, 2, B], F32)
        silu2 = sb("silu2", [P, 2, B], F32)
        wx = sb("wx", [D, D], F32)
        wh = sb("wh", [D, D], F32)
        rb_c = sb("rb_c", [P, 1], F32)
        wr = sb("wr", [D, E0], F32)
        br_b = sb("br_b", [P, E0], F32)
        rows = sb("rows", [ROWS, P], F32)
        cols = sb("cols", [P, ROWS], F32)
        cgw_s = sb("cgw_s", [P, 3, EC], F32)
        cgb_b = sb("cgb_b", [P, EC], F32)
        ctw_s = sb("ctw_s", [P, 2 * EC], F32)
        ctb_b = sb("ctb_b", [P, 2 * EC], F32)
        mod = sb("mod", [P, 2 * EC], F32)
        agg_s = sb("agg_s", [P, 3, B], F32)
        agg_t = sb("agg_t", [P, 3, B], F32)
        agg = sb("agg", [P, 3, 2, B], F32)
        la = sb("la", [P, EC], F32)
        wsum = sb("wsum", [P, 1], F32)
        wrec = sb("wrec", [P, 1], F32)
        wbe = sb("wbe", [P, EC], F32)
        be2 = sb("be2", [GW, D], F32)
        be2_r1 = sb("be2_r1", [GW, D], F32)
        be2_r2 = sb("be2_r2", [GW, D], F32)
        be2_p = sb("be2_p", [3 * GW, 3, D], BF16)

        bias0_cur = sb("bias0_cur", [P, 2], F32)
        bias_cur = sb("bias_cur", [P, FC], F32)

        ps = ctx.enter_context(nc.psum_tensor("ps", [P, 8, 512], F32))
        bank = lambda n: ps[:, n, :]
        pair = lambda n: ps[:, n:n + 2, :].rearrange("p a b -> p (a b)")
        GT_BANK = ps[0:3 * GW, 3, :].bitcast(BF16)

        s_x = [sem(f"s_xq{q}") for q in range(4)]
        s_rnnw = sem("s_rnnw")
        s_rt = sem("s_rt")
        s_small = sem("s_small")
        s_w0 = sem("s_w0")
        s_wc = sem("s_wc")
        s_wf = sem("s_wf")
        s_out = sem("s_out")
        s_zero = sem("s_zero")
        s_id = sem("s_id")
        s_const = sem("s_const")
        s_condp = sem("s_condp")
        s_cond = sem("s_cond")
        s_xp = sem("s_xp")
        s_xt = sem("s_xt")
        s_rowp = sem("s_rowp")
        s_cols = sem("s_cols")
        s_silue = sem("s_silue")
        s_silu = sem("s_silu")
        s_modp = sem("s_modp")
        s_mod = sem("s_mod")
        s_be2 = sem("s_be2")
        s_step = sem("s_step")
        s_h = sem("s_h")
        s_inhi = sem("s_inhi")
        s_inlo = sem("s_inlo")
        s_res = sem("s_res")
        s_lgp = sem("s_lgp")
        s_lg = sem("s_lg")
        s_shift = sem("s_shift")
        s_ex = sem("s_ex")
        s_g3 = sem("s_g3")
        s_gTp = sem("s_gTp")
        s_gT = sem("s_gT")
        s_v = sem("s_v")
        s_w1hi0 = sem("s_w1hi0")
        s_w1lo0 = sem("s_w1lo0")
        s_w2hi0 = sem("s_w2hi0")
        s_w2lo0 = sem("s_w2lo0")
        s_z0 = sem("s_z0")
        s_g0 = sem("s_g0")
        s_hid0 = sem("s_hid0")
        s_hg0 = sem("s_hg0")
        s_hi0 = sem("s_hi0")
        s_lo0 = sem("s_lo0")
        s_y0 = sem("s_y0")
        s_x1 = sem("s_x1")
        s_x1hi = sem("s_x1hi")
        s_x1lo = sem("s_x1lo")
        s_b0 = sem("s_b0")
        s_b = sem("s_b")
        s_wv = sem("s_wv")
        s_wp = sem("s_wp")
        s_full = sem("s_full")
        s_hid = sem("s_hid")
        s_free = sem("s_free")
        s_lo = sem("s_lo")
        s_y = sem("s_y")
        s_yg = sem("s_yg")
        s_acc = sem("s_acc")
        s_agg = sem("s_agg")
        s_gc = sem("s_gc")
        s_c = sem("s_c")
        s_chi = sem("s_chi")
        s_clo = sem("s_clo")
        s_fin = sem("s_fin")
        s_outp = sem("s_outp")
        s_nat = sem("s_nat")

        SLOTS_C = sum(len(SLOTS["c", e == 0]) for e in range(NC_))
        ITEMS_C = NC_ * 2 * FC
        N_ITEMS0 = N0 * J0
        GC = h_f

        block = ctx.enter_context(nc.Block())
        x_v = x.rearrange("b (i s) d -> s b i d", s=2)
        out_v = out.rearrange("b (i s) d -> s b i d", s=2)

        def slot_base(phase, e):
            if isinstance(e, int) and e == 0:
                return 0 if phase == "c" else SLOTS_C
            usual, first = len(SLOTS[phase, False]), len(SLOTS[phase, True])
            return e * usual + ((0 if phase == "c" else SLOTS_C) + first - usual)

        def item_base(phase, e):
            return e * (2 * FC) + (0 if phase == "c" else ITEMS_C)

        def yg_base(phase, e):
            return e * 2 + (0 if phase == "c" else 2 * NC_)

        def experts(eng, count, body):
            body(0, True, False)
            with eng.Fori(1, count - 1) as e:
                body(e, False, False)
            body(count - 1, False, True)

        def last_of(phase, e):
            return ("c", NC_ - 1) if phase == "f" and isinstance(e, int) and e == 0 else (phase, e - 1)

        def sees(phase, e, j):
            return SEES[e][j] if phase == "c" else (0, C1)

        def acc_base(phase, e):
            return e * 2 + (0 if phase == "c" else 2 * (NC_ - 1))

        @block.sync
        def _(sp):
            def quarter(q):
                for s in range(2):
                    sp.dma_start(nat[64 * s:64 * s + 64, 4 * q:4 * q + 4, :],
                                 x_v[s, :, 4 * q:4 * q + 4, :]).then_inc(s_x[q], 16)
            sp.dma_start(cond_n[:], cond).then_inc(s_rnnw, 16)
            quarter(0)
            sp.dma_start(wh[:], Wh).then_inc(s_rnnw, 16)
            sp.dma_start(wr[:], Wr).then_inc(s_rt, 16)
            sp.dma_start(br_b[:], br.partition_broadcast(P)).then_inc(s_rt, 16)
            for q in range(1, 4):
                quarter(q)
            small = [(rows[R_B0:R_B0 + E0, :], Be1), (rows[R_B0 + E0:R_BC, :], bs1.unsqueeze(0)),
                     (rows[R_BC:R_BC + FC, :], sb1.rearrange("(c p) -> c p", p=P)),
                     (rows[R_BC + FC:R_BF, :], eb1.rearrange("e (c p) -> (e c) p", p=P)),
                     (rows[R_BF:R_YC, :], fb1.rearrange("e (c p) -> (e c) p", p=P)),
                     (rows[R_YC:R_YC + 1, :], sb2.unsqueeze(0)), (rows[R_YC + 1:R_YF, :], eb2),
                     (rows[R_YF:R_GF, :], fb2), (rows[R_GF:ROWS, :], fgw),
                     (be2[0:E0, :], Be2), (be2[E0:N0, :], bs2.unsqueeze(0)),
                     (ctw_s[:], ctw), (ctb_b[:], ctb.partition_broadcast(P)),
                     (cgw_s[:], cgw.rearrange("(k p) e -> p k e", p=P)), (cgb_b[:], cgb.partition_broadcast(P))]
            assert len(small) == N_SMALL
            for dst, src in small:
                sp.dma_start(dst, src).then_inc(s_small, 16)
            for dst, routed, shared in ((raw1, We1, ws1), (raw2, We2, ws2)):
                d = dst[:].rearrange("p (e f) -> p e f", f=D)
                sp.dma_start(d[:, 0:E0, :], routed.rearrange("e k f -> k e f")).then_inc(s_w0, 16)
                sp.dma_start(d[:, E0, :], shared).then_inc(s_w0, 16)
            d = rawc1[:].rearrange("p (e f) -> p e f", e=NC_)
            sp.dma_start(d[:, 0, :], sw1).then_inc(s_wc, 16)
            sp.dma_start(d[:, 1:NC_, :], ew1.rearrange("e k f -> k e f")).then_inc(s_wc, 16)
            d = rawc2[:].rearrange("p (e c f) -> p e c f", e=NC_, c=FC)
            sp.dma_start(d[:, 0, :, :], sw2.rearrange("(c p) f -> p c f", p=P)).then_inc(s_wc, 16)
            for e in range(EC):
                sp.dma_start(d[:, 1 + e, :, :], ew2[e].rearrange("(c p) f -> p c f", p=P)).then_inc(s_wc, 16)
            sp.wait_ge(s_w1lo0, N0)
            sp.wait_ge(s_w2lo0, N0)
            sp.dma_start(raw1[:].rearrange("p (e f) -> p e f", e=EF),
                         fw1.rearrange("e k f -> k e f")).then_inc(s_wf, 16)
            d = raw2[:].rearrange("p (e c f) -> p e c f", e=EF, c=FC)
            for e in range(EF):
                sp.dma_start(d[:, e, :, :], fw2[e].rearrange("(c p) f -> p c f", p=P)).then_inc(s_wf, 16)
            for j in range(J1):
                sp.wait_ge(s_nat, j + 1)
                for s in range(2):
                    sp.dma_start(out_v[s, :, 8 * j:8 * j + 8, :],
                                 nat[64 * s:64 * s + 64, 8 * j:8 * j + 8, :]).then_inc(s_out, 16)
            sp.wait_ge(s_out, 16 * 2 * J1)

        @block.gpsimd
        def _(pool):
            nc.gpsimd.memset(ident[:], 0.0).then_inc(s_zero, 1)
            pool.wait_ge(s_zero, 1)
            nc.gpsimd.affine_select(out=ident[:], in_=ident[:], compare_op=ALU.not_equal, fill=1.0, base=0,
                                    pattern=[[-1, P]], channel_multiplier=1).then_inc(s_id, 1)
            for tab in (lg0, take8, lgc, lgf, take8c, take8f):
                nc.gpsimd.memset(tab[:], NEG).then_inc(s_const, 1)
            nc.gpsimd.memset(gates[:], 0.0).then_inc(s_const, 1)
            nc.gpsimd.memset(ident_b[:], 0.0).then_inc(s_zero, 1)
            nc.gpsimd.memset(pick[:], 0.0).then_inc(s_zero, 1)
            pool.wait_ge(s_zero, 3)
            nc.gpsimd.affine_select(out=ident_b[:], in_=ident_b[:], compare_op=ALU.not_equal, fill=1.0, base=0,
                                    pattern=[[-1, P]], channel_multiplier=1).then_inc(s_id, 1)
            for k in range(3):
                nc.gpsimd.affine_select(out=pick[:], in_=pick[:], compare_op=ALU.not_equal, fill=1.0,
                                        base=-GW * k, pattern=[[-1, GW], [0, P]],
                                        channel_multiplier=1).then_inc(s_zero, 1)
                pool.wait_ge(s_zero, 4 + k)
            pool.wait_ge(s_const, 7)
            nc.gpsimd.memset(gates[:, :, E0:N0], 1.0).then_inc(s_const, 1)
            nc.gpsimd.memset(c_f[:], 0.0).then_inc(s_const, 1)

            def lo0(e, par, which):
                raw, hi, lo, s_hi, s_lo = ((raw1, w1h0, w1l0, s_w1hi0, s_w1lo0),
                                           (raw2, w2h0, w2l0, s_w2hi0, s_w2lo0))[which]
                pool.wait_ge(s_hi, e + 1)
                nc.gpsimd.tensor_tensor(lo[:, par, :], raw[:, bass.ds(e * D, D)], hi[:, par, :].bitcast(F32),
                                        ALU.subtract).then_inc(s_lo, 1)
            for q in range(4):
                cut = slice(q * C0, (q + 1) * C0)
                pool.wait_ge(s_inhi, q + 1)
                nc.gpsimd.tensor_tensor(in_lo[:, cut], h_f[:, cut], in_hi[:, cut].bitcast(F32),
                                        ALU.subtract).then_inc(s_inlo, 1)
                if q == 2:
                    lo0(0, 0, 0)
                    lo0(0, 0, 1)
            lo0(1, 1, 0)
            for q in range(4):
                cut = slice(q * C0, (q + 1) * C0)
                pool.wait_ge(s_h, T)
                nc.gpsimd.tensor_tensor(x_f[:, cut], x_f[:, cut], h_f[:, cut], ALU.add).then_inc(s_res, 1)
                if q == 1:
                    lo0(1, 1, 1)
            with pool.Fori(1, N0 // 2) as i:
                lo0(i * 2, 0, 0)
                lo0(i * 2, 0, 1)
                lo0(i * 2 + 1, 1, 0)
                lo0(i * 2 + 1, 1, 1)

            def w_lo(half, e, raws, count):
                hi, lo, raw = ((w1h, w1l, raws[0]), (w2h, w2l, raws[1]))[half // 2]
                at = half % 2 * 2 * P
                pool.wait_ge(s_wv, count)
                nc.gpsimd.tensor_tensor(lo[:, at:at + 2 * P], raw[:, bass.ds(e * (FC * P) + at, 2 * P)],
                                        hi[:, at:at + 2 * P].bitcast(F32), ALU.subtract).then_inc(s_wp, 1)

            def add(phase, e, j):
                acc = c_f if phase == "c" else x_f
                lo, hi = sees(phase, e, j)
                cut = slice(j * C1 + lo, j * C1 + hi)
                pool.wait_ge(s_yg, yg_base(phase, e) + j + 1)
                nc.gpsimd.tensor_tensor(acc[:, cut], acc[:, cut], yg[:, j, lo:hi], ALU.add).then_inc(s_acc, 1)

            for half in range(4):
                w_lo(half, 0, (rawc1, rawc2), half + 1)

            def body(phase):
                raws = (rawc1, rawc2) if phase == "c" else (raw1, raw2)
                wbase = 0 if phase == "c" else 4 * NC_

                def one(e, first, last):
                    late = phase == "f" and first
                    if not (phase == "c" and first):
                        w_lo(3, e, raws, e * 4 + (wbase + 4))
                    if not first:
                        add(phase, e - 1, 1)
                    if not last and not late:
                        add(phase, e, 0)
                    if not last or phase == "c":
                        nxt, src = (0, (raw1, raw2)) if last else (e + 1, raws)
                        for half in range(3):
                            w_lo(half, nxt, src, e * 4 + (wbase + 4 + half + 1))
                    if late:
                        add(phase, e, 0)
                return one
            for e in range(NC_):
                body("c")(e, e == 0, e == NC_ - 1)
            experts(pool, EF, body("f"))

        @block.scalar
        def _(act):
            act.dma_start(wx[:], Wx).then_inc(s_rnnw, 16)
            act.dma_start(rb_c[:], rb.unsqueeze(1)).then_inc(s_rnnw, 16)
            act.wait_ge(s_cond, 2)
            nc.scalar.activation(silu_e[:], cond2[:], ACT.Exp, scale=-1.0).then_inc(s_silue, 1)

            def route_exp(q, cut, n, shifts):
                act.wait_ge(s_shift, shifts)
                nc.scalar.activation(ex[:, cut, 0:n], g_r1[:, cut, 0:n], ACT.Exp).then_inc(s_ex, 1)

            def w_hi0(par, cut, which):
                raw, hi, s = ((raw1, w1h0, s_w1hi0), (raw2, w2h0, s_w2hi0))[which]
                act.wait_ge(s_w0, 64)
                nc.scalar.activation(hi[:, par, :], raw[:, cut], ACT.Copy).then_inc(s, 1)

            act.wait_ge(s_rnnw, 64)
            for t in range(T):
                act.wait_ge(s_step, t + 1)
                nc.scalar.activation(h_f[:, t * B:(t + 1) * B], ps[:, t % 2, 0:B], ACT.Tanh,
                                     bias=rb_c[:, 0:1]).then_inc(s_h, 1)
                if t % 8 == 5 and t > 8:
                    q = t // 8 - 1
                    route_exp(q, slice(4 * q, 4 * q + 4), E0, q + 1)
                if t == T - 2:
                    w_hi0(0, slice(0, D), 0)
                    w_hi0(0, slice(0, D), 1)

            def item0(n, i, m, last):
                e_par, j = m // J0, m % J0
                act.wait_ge(s_z0, n + 1)
                if not (isinstance(n, int) and n < 2):
                    act.wait_ge(s_hg0, n - 1)
                e = i * 2 + e_par
                if j == 0:
                    act.wait_ge(s_b0, e + 1)
                nc.scalar.activation(hid[:, m % 2, 0:C0], bank(4 + m % 2), ACT.Gelu,
                                     bias=bias0_cur[:, e_par:e_par + 1]).then_inc(s_hid0, 1)
                if isinstance(n, int) and n == 1:
                    route_exp(3, slice(12, 16), E0, 4)
                if not (isinstance(n, int) and n == 0):
                    hi0(n - 1, (m - 1) % 8)
                if j == 0 and not (isinstance(n, int) and n == 0):
                    w_hi0(e_par, bass.ds(e * D, D), 1)
                if j == 0 and not (last and e_par == 1):
                    w_hi0(1 - e_par, bass.ds(e * D + D, D), 0)

            def hi0(n, m):
                act.wait_ge(s_hg0, n + 1)
                if not (isinstance(n, int) and n < 4):
                    act.wait_ge(s_y0, n - 3)
                nc.scalar.activation(hid_hi[:, m % 4, 0:C0], yg[:, m % 2, 0:C0], ACT.Copy).then_inc(s_hi0, 1)

            def pair0(i, first, last):
                for m in range(2 * J0):
                    item0(i * (2 * J0) + m, i, m, last)
            experts(act, N0 // 2, pair0)
            hi0(N_ITEMS0 - 1, 2 * J0 - 1)

            for q in range(4):
                cut = slice(q * C0, (q + 1) * C0)
                act.wait_ge(s_x1, q + 1)
                nc.scalar.activation(in_hi[:, cut], x_f[:, cut], ACT.Copy).then_inc(s_x1hi, 1)

            def c_hi(j):
                cut = slice(j * C1, (j + 1) * C1)
                act.wait_ge(s_c, j + 1)
                nc.scalar.activation(in_hi[:, cut], c_f[:, cut], ACT.Copy).then_inc(s_chi, 1)

            def body(phase):
                func = ACT.Gelu_apprx_tanh if phase == "c" else ACT.Relu

                def one(e, first, last):
                    n = 0
                    for k, (kind, j, f) in enumerate(SLOTS[phase, first]):
                        S = slot_base(phase, e) + k
                        lo, hi = sees(phase, e, j)
                        src = pair(4 + 2 * (k % 2))
                        act.wait_ge(s_full, S + 1)
                        if kind == "F":
                            item = item_base(phase, e) + n
                            bias = bias_cur[:, f:f + 1]
                            if j == 0 and f in (0, 2):
                                act.wait_ge(s_b, (e * 2 + (f // 2 + 1)) + (0 if phase == "c" else 2 * NC_))
                            if not (phase == "c" and first and n < 2):
                                act.wait_ge(s_lo, item - 1)
                            nc.scalar.activation(hid[:, n % 2, lo:hi], src[:, lo:hi], func,
                                                 bias=bias).then_inc(s_hid, 1)
                            if not (phase == "c" and first and n < 4):
                                act.wait_ge(s_y, item - 3)
                            nc.scalar.activation(hid_hi[:, n % 4, lo:hi], src[:, lo:hi], func,
                                                 bias=bias).then_inc(s_free, 1)
                            n += 1
                        elif kind == "G":
                            act.wait_ge(s_yg, yg_base(phase, e) + (j - 1))
                            nc.scalar.activation(GC[:, j * C1:(j + 1) * C1], src, ACT.Copy).then_inc(s_free, 1)
                        elif kind == "A":
                            nc.scalar.activation(la[:], src[:, 0:EC], ACT.Copy).then_inc(s_free, 1)
                        elif kind == "R":
                            nc.scalar.activation(lgf[:, :, 0:EF],
                                                 src[:, 0:TILES * EF].rearrange("p (i e) -> p i e", e=EF),
                                                 ACT.Copy).then_inc(s_free, 1)
                        elif phase == "c":
                            nc.scalar.activation(gc_T[:].rearrange("p e b -> p (e b)"), src[:, 0:EC * B],
                                                 ACT.Copy).then_inc(s_free, 1)
                        else:
                            nc.scalar.activation(gates_T[:], src[0:3 * GW, :].bitcast(BF16),
                                                 ACT.Copy).then_inc(s_free, 1)
                        if phase == "c" and first and k == 6:
                            act.wait_ge(s_shift, 5)
                            nc.scalar.activation(ex[:, 0:1, 0:EC], g_r1[:, 0:1, 0:EC], ACT.Exp).then_inc(s_ex, 1)
                        if phase == "c" and last and k == 5:
                            c_hi(0)
                        if phase == "f" and first and k == 1:
                            c_hi(1)
                        if phase == "f" and first and k == 5:
                            act.wait_ge(s_shift, 6)
                            nc.scalar.activation(ex[:, :, 0:EF], g_r1[:, :, 0:EF], ACT.Exp).then_inc(s_ex, 1)
                return one
            for e in range(NC_):
                body("c")(e, e == 0, e == NC_ - 1)
            experts(act, EF, body("f"))
            for j in range(J1):
                act.wait_ge(s_outp, j + 1)
                nc.scalar.activation(nat[:, 8 * j:8 * j + 8, :], pair(4 + 2 * j).rearrange("p (i d) -> p i d", d=D),
                                     ACT.Copy).then_inc(s_nat, 1)

        @block.vector
        def _(dve):
            chain = [0]

            def link(ins):
                chain[0] += 1
                ins.then_inc(s_v, 1)
                dve.wait_ge(s_v, chain[0])

            V = nc.vector
            dve.wait_ge(s_condp, 1)
            for k in range(2):
                V.tensor_copy(cond2[:, k, :], ps[:, 6, 0:B]).then_inc(s_cond, 1)
            for q in range(4):
                dve.wait_ge(s_xp, q + 1)
                V.tensor_copy(x_f[:, q * C0:(q + 1) * C0], bank(4 + q % 2)).then_inc(s_xt, 1)
            dve.wait_ge(s_silue, 1)
            link(V.tensor_scalar(silu_e[:], silu_e[:], 1.0, None, ALU.add))
            link(V.reciprocal(silu_e[:], silu_e[:]))
            V.tensor_tensor(silu2[:], cond2[:], silu_e[:], ALU.mult).then_inc(s_silu, 1)

            def biases_and_modulation():
                dve.wait_ge(s_rowp, 1)
                V.tensor_copy(cols[:], ps[:, 6, 128:128 + ROWS]).then_inc(s_cols, 1)
                dve.wait_ge(s_small, 16 * N_SMALL)
                dve.wait_ge(s_modp, 1)
                V.tensor_tensor(mod[:], ps[:, 6, 256:256 + 2 * EC], ctb_b[:], ALU.add).then_inc(s_mod, 1)
                dve.wait_ge(s_mod, 1)
                V.tensor_scalar(mod[:, 0:EC], mod[:, 0:EC], 1.0, None, ALU.add).then_inc(s_mod, 1)
                link(V.tensor_copy(be2_p[0:GW, 0, :], be2[:]))
                link(V.tensor_tensor(be2_r1[:], be2[:], be2_p[0:GW, 0, :], ALU.subtract))
                link(V.tensor_copy(be2_p[0:GW, 1, :], be2_r1[:]))
                link(V.tensor_tensor(be2_r2[:], be2_r1[:], be2_p[0:GW, 1, :], ALU.subtract))
                link(V.tensor_copy(be2_p[0:GW, 2, :], be2_r2[:]))
                for k in range(1, 3):
                    V.tensor_copy(be2_p[GW * k:GW * (k + 1), :, :], be2_p[0:GW, :, :]).then_inc(s_be2, 1)

            def topk(lg, tiles, n, k, take, part, pad):
                if part == 0:
                    for i in tiles:
                        V.max(top8[:, i, :], lg[:, i, 0:max(n, 8)]).then_inc(s_v, 1)
                        chain[0] += 1
                    dve.wait_ge(s_v, chain[0])
                    cut = slice(tiles[0], tiles[-1] + 1)
                    link(V.tensor_copy(take[:, cut, 0:k], top8[:, cut, 0:k]))
                else:
                    for i in tiles:
                        V.match_replace(left[:, i, 0:pad], take[:, i, :], lg[:, i, 0:pad], TAKEN).then_inc(s_v, 1)
                        chain[0] += 1
                    dve.wait_ge(s_v, chain[0])

            def shift(lg, tiles, n):
                cut = slice(tiles[0], tiles[-1] + 1)
                link(V.tensor_tensor(taken[:, cut, 0:n], left[:, cut, 0:n], lg[:, cut, 0:n], ALU.not_equal))
                V.tensor_tensor(g_r1[:, cut, 0:n], lg[:, cut, 0:n],
                                top8[:, cut, 0:1].broadcast_to([P, len(tiles), n]),
                                ALU.subtract).then_inc(s_shift, 1)

            def softmax(tiles, n, exs, out_g):
                cut = slice(tiles[0], tiles[-1] + 1)
                dve.wait_ge(s_ex, exs)
                link(V.tensor_reduce(ssum[:, cut], ex[:, cut, 0:n], AX, ALU.add))
                link(V.reciprocal(rsum[:, cut], ssum[:, cut]))
                link(V.tensor_tensor(ex[:, cut, 0:n], ex[:, cut, 0:n], taken[:, cut, 0:n], ALU.mult))
                link(V.tensor_tensor(out_g, ex[:, cut, 0:n],
                                     rsum[:, cut].unsqueeze(2).broadcast_to([P, len(tiles), n]), ALU.mult))

            def split3(tiles, n):
                cut = slice(tiles[0], tiles[-1] + 1)
                part = [gates3[:, cut, GW * k:GW * k + n] for k in range(3)]
                link(V.tensor_copy(part[0], gates[:, cut, 0:n]))
                link(V.tensor_tensor(g_r1[:, cut, 0:n], gates[:, cut, 0:n], part[0], ALU.subtract))
                link(V.tensor_copy(part[1], g_r1[:, cut, 0:n]))
                link(V.tensor_tensor(g_r2[:, cut, 0:n], g_r1[:, cut, 0:n], part[1], ALU.subtract))
                V.tensor_copy(part[2], g_r2[:, cut, 0:n]).then_inc(s_g3, 1)

            def gates_T_out(q):
                dve.wait_ge(s_gTp, q + 1)
                V.tensor_copy(gates_T[:, q * C0:(q + 1) * C0],
                              GT_BANK[:, q % 2 * C0:(q % 2 + 1) * C0]).then_inc(s_gT, 1)

            def w_hi(half, e, raws):
                hi, raw = ((w1h, raws[0]), (w2h, raws[1]))[half // 2]
                at = half % 2 * 2 * P
                V.tensor_copy(hi[:, at:at + 2 * P], raw[:, bass.ds(e * (FC * P) + at, 2 * P)]).then_inc(s_wv, 1)

            def route0(q, part):
                tiles = list(range(4 * q, 4 * q + 4))
                if part == 0:
                    dve.wait_ge(s_lgp, q + 1)
                    V.tensor_tensor(lg0[:, 4 * q:4 * q + 4, 0:E0],
                                    ps[:, 2, 128 * q:128 * q + 128].rearrange("p (i e) -> p i e", e=GW)[:, :, 0:E0],
                                    br_b[:].unsqueeze(1).broadcast_to([P, 4, E0]), ALU.add).then_inc(s_lg, 1)
                    dve.wait_ge(s_lg, q + 1)
                    topk(lg0, tiles, E0, K0, take8, 0, 0)
                    topk(lg0, tiles, E0, K0, take8, 1, E0 + 9)
                    shift(lg0, tiles, E0)
                else:
                    softmax(tiles, E0, q + 1, gates[:, 4 * q:4 * q + 4, 0:E0])
                    split3(tiles, GW)

            dve.wait_ge(s_const, 8)
            for q in range(4):
                dve.wait_ge(s_h, 8 * q + 8)
                cut = slice(q * C0, (q + 1) * C0)
                V.tensor_copy(in_hi[:, cut], h_f[:, cut]).then_inc(s_inhi, 1)
                route0(q, 0)
                if q < 3:
                    route0(q, 1)
                    gates_T_out(q)
                if q == 1:
                    biases_and_modulation()
                if q == 2:
                    dve.wait_ge(s_wc, 16 * N_WC)
                    for half in range(4):
                        w_hi(half, 0, (rawc1, rawc2))

            def bias0(e, par):
                V.tensor_scalar(bias0_cur[:, par:par + 1], cols[:, bass.ds(e + R_B0, 1)], 0.0, None,
                                ALU.add).then_inc(s_b0, 1)

            def bias1(phase, e, half):
                at = e * FC + ((R_BC if phase == "c" else R_BF) + 2 * half)
                V.tensor_scalar(bias_cur[:, 2 * half:2 * half + 2], cols[:, bass.ds(at, 2)], 0.0, None,
                                ALU.add).then_inc(s_b, 1)

            def hg0(n, m):
                dve.wait_ge(s_hid0, n + 1)
                dve.wait_ge(s_g0, n + 1)
                if not (isinstance(n, int) and n < 2):
                    dve.wait_ge(s_lo0, n - 1)
                V.tensor_tensor(yg[:, m % 2, 0:C0], hid[:, m % 2, 0:C0], bank(6 + m % 2), ALU.mult).then_inc(s_hg0, 1)

            def lo0(n, m):
                dve.wait_ge(s_hi0, n + 1)
                V.tensor_tensor(hid_lo[:, m % 4, 0:C0], yg[:, m % 2, 0:C0], hid_hi[:, m % 4, 0:C0].bitcast(F32),
                                ALU.subtract).then_inc(s_lo0, 1)

            def pair0(i, first, last):
                for m in range(2 * J0):
                    n = i * (2 * J0) + m
                    if first and m == 3:
                        gates_T_out(3)
                    hg0(n, m)
                    if not (first and m == 0):
                        lo0(n - 1, (m - 1) % 8)
                    if first and m == 1:
                        route0(3, 1)
                    if m % J0 == 0 and not (last and m == J0):
                        bias0(i * 2 + (m // J0 + 1), 1 - m // J0)
            bias0(0, 0)
            bias1("c", 0, 0)
            bias1("c", 0, 1)
            experts(dve, N0 // 2, pair0)
            lo0(N_ITEMS0 - 1, 2 * J0 - 1)


            def x1_lo(q):
                cut = slice(q * C0, (q + 1) * C0)
                dve.wait_ge(s_x1hi, q + 1)
                V.tensor_tensor(in_lo[:, cut], x_f[:, cut], in_hi[:, cut].bitcast(F32), ALU.subtract).then_inc(s_x1lo, 1)
            for q in range(4):
                cut = slice(q * C0, (q + 1) * C0)
                dve.wait_ge(s_res, q + 1)
                dve.wait_ge(s_y0, N_ITEMS0 - J0 + q + 1)
                V.tensor_tensor(x_f[:, cut], x_f[:, cut], bank(q), ALU.add).then_inc(s_x1, 1)
                if q:
                    x1_lo(q - 1)
            x1_lo(3)

            def means(part):
                seg = x_f[:].rearrange("p (t b) -> p b t", b=B)
                cuts = (slice(0, T_HEAD), slice(T_HEAD, T_HEAD + T_WRIST), slice(T_HEAD + T_WRIST, T))
                if part < 3:
                    if part == 0:
                        dve.wait_ge(s_x1, 4)
                    V.tensor_reduce(agg_s[:, part, :], seg[:, :, cuts[part]], AX, ALU.add).then_inc(s_v, 1)
                    chain[0] += 1
                    return
                dve.wait_ge(s_v, chain[0])
                head, wrist, prop = (agg_s[:, k, :] for k in range(3))
                link(V.tensor_tensor(agg_t[:, 1, :], head, prop, ALU.add))
                link(V.tensor_tensor(agg_t[:, 2, :], wrist, prop, ALU.add))
                link(V.tensor_tensor(agg_t[:, 0, :], agg_t[:, 1, :], wrist, ALU.add))
                for k, count in enumerate((T, T - T_WRIST, T - T_HEAD)):
                    V.tensor_scalar(agg[:, k, :, :], agg_t[:, k, :].unsqueeze(1).broadcast_to([P, 2, B]),
                                    1.0 / count, None, ALU.mult).then_inc(s_agg, 1)

            def gate_c(part):
                if part == 0:
                    dve.wait_ge(s_free, 5)
                    dve.wait_ge(s_mod, 2)
                    link(V.tensor_tensor(la[:], la[:], cgb_b[:], ALU.add))
                    link(V.tensor_tensor(la[:], la[:], mod[:, 0:EC], ALU.mult))
                    link(V.tensor_tensor(lgc[:, 0, 0:EC], la[:], mod[:, EC:2 * EC], ALU.add))
                    topk(lgc, [0], EC, KC, take8c, 0, 0)
                    topk(lgc, [0], EC, KC, take8c, 1, 16)
                    shift(lgc, [0], EC)
                elif part == 1:
                    softmax([0], EC, 5, wbe[:].unsqueeze(1))
                    link(V.tensor_reduce(wsum[:], wbe[:], AX, ALU.add))
                    link(V.tensor_scalar(wsum[:], wsum[:], 1e-8, None, ALU.add))
                    link(V.reciprocal(wrec[:], wsum[:]))
                    link(V.tensor_scalar(wbe[:], wbe[:], wrec[:, 0:1], None, ALU.mult))
                    V.tensor_copy(gc_w[:], wbe[0:B, :].unsqueeze(2).broadcast_to([B, EC, P])).then_inc(s_gc, 1)

            def route_f(part):
                tiles = list(range(TILES))
                if part == 0:
                    dve.wait_ge(s_free, SLOTS_C + 3)
                    topk(lgf, tiles, EF, KF, take8f, 0, 0)
                elif part == 1:
                    topk(lgf, tiles, EF, KF, take8f, 1, 16)
                    shift(lgf, tiles, EF)
                else:
                    softmax(tiles, EF, 6, gates[:, :, 0:EF])
                    split3(tiles, EF)

            def evac(phase, e, j, late=False):
                bias = cols[:, bass.ds(e + (R_YC if phase == "c" else R_YF), 1)]
                lo, hi = sees(phase, e, j)
                dve.wait_ge(s_y, item_base(phase, e) + (4 * j + 4))
                if phase == "c" and e == 0:
                    V.tensor_scalar(yg[:, j, lo:hi], pair(2 * j)[:, lo:hi], bias, None, ALU.add).then_inc(s_yg, 1)
                    return
                if phase == "f" and isinstance(e, int) and e == 0:
                    dve.wait_ge(s_c, 2)
                else:
                    dve.wait_ge(s_acc, acc_base(phase, e) + (j - 1))
                if phase == "c":
                    dve.wait_ge(s_free, len(SLOTS["c", True]))
                    n = (hi - lo) // B
                    V.scalar_tensor_tensor(yg[:, j, lo:hi].rearrange("p (t b) -> p t b", b=B),
                                           pair(2 * j)[:, lo:hi].rearrange("p (t b) -> p t b", b=B), bias,
                                           gc_T[:, e - 1, :].unsqueeze(1).broadcast_to([P, n, B]),
                                           ALU.add, ALU.mult).then_inc(s_yg, 1)
                    return
                slot = slot_base(phase, e) + (len(SLOTS["f", late]) if j or late else 5)
                if late and j == 0:
                    slot = slot - 2
                dve.wait_ge(s_free, slot)
                V.scalar_tensor_tensor(yg[:, j, :], pair(2 * j), bias, GC[:, j * C1:(j + 1) * C1],
                                       ALU.add, ALU.mult).then_inc(s_yg, 1)

            def total(phase, j):
                count = NC_ if phase == "c" else EF
                acc, s = (c_f, s_c) if phase == "c" else (x_f, s_fin)
                cut = slice(j * C1, (j + 1) * C1)
                dve.wait_ge(s_yg, yg_base(phase, count - 1) + j + 1)
                dve.wait_ge(s_acc, acc_base(phase, count - 1) + (j - 1))
                V.tensor_tensor(acc[:, cut], acc[:, cut], yg[:, j, :], ALU.add).then_inc(s, 1)

            def c_lo(j):
                cut = slice(j * C1, (j + 1) * C1)
                dve.wait_ge(s_chi, j + 1)
                V.tensor_tensor(in_lo[:, cut], c_f[:, cut], in_hi[:, cut].bitcast(F32), ALU.subtract).then_inc(s_clo, 1)

            def body(phase):
                raws = (rawc1, rawc2) if phase == "c" else (raw1, raw2)

                def one(e, first, last):
                    base = slot_base(phase, e)
                    late = phase == "f" and first
                    nxt, src = (0, (raw1, raw2)) if last else (e + 1, raws)
                    prefetch = not (last and phase == "f")
                    n = 0
                    for k, (kind, j, f) in enumerate(SLOTS[phase, first]):
                        if kind != "F":
                            continue
                        lo, hi = sees(phase, e, j)
                        dve.wait_ge(s_free, base + (k + 1))
                        V.tensor_tensor(hid_lo[:, n % 4, lo:hi], hid[:, n % 2, lo:hi],
                                        hid_hi[:, n % 4, lo:hi].bitcast(F32), ALU.subtract).then_inc(s_lo, 1)
                        n += 1
                        if (j, f) == (0, 0) and not (phase == "c" and first):
                            dve.wait_ge(s_y, item_base(phase, e))
                            w_hi(3, e, raws)
                            before = last_of(phase, e)
                            evac(*before, 1)
                            if late:
                                total("c", 1)
                        if late and (j, f) == (0, 1):
                            c_lo(1)
                        if late and (j, f) in ((0, 2), (0, 3), (1, 0)):
                            route_f({(0, 2): 0, (0, 3): 1, (1, 0): 2}[j, f])
                        if phase == "c" and first and (j, f) == (0, 0):
                            means(0)
                            means(1)
                        if phase == "c" and first and (j, f) == (0, 1):
                            means(2)
                            means(3)
                        if (j, f) == (1, 0):
                            if not late:
                                evac(phase, e, 0)
                            if last:
                                total(phase, 0)
                            if phase == "c" and first:
                                gate_c(0)
                        if (j, f) == (1, 1):
                            if prefetch and last:
                                dve.wait_ge(s_wf, 16 * N_WF)
                            if prefetch:
                                w_hi(0, nxt, src)
                                bias1("f" if last else phase, nxt, 0)
                            if phase == "c" and first:
                                gate_c(1)
                        if phase == "c" and last and (j, f) == (1, 2):
                            c_lo(0)
                        if (j, f) == (1, 3) and prefetch:
                            w_hi(1, nxt, src)
                            bias1("f" if last else phase, nxt, 1)
                            dve.wait_ge(s_y, item_base(phase, e) + (4 + 2))
                            w_hi(2, nxt, src)
                    if late:
                        evac(phase, e, 0, late=True)
                    if last and phase == "f":
                        evac(phase, e, 1)
                        total(phase, 1)
                return one
            for e in range(NC_):
                body("c")(e, e == 0, e == NC_ - 1)
            experts(dve, EF, body("f"))

        @block.tensor
        def _(pe):
            M = nc.tensor

            def pick_of(e):
                return pick[:].rearrange("p e m -> p (e m)")[:, bass.ds(e * P, P)]

            def mm3(o, wts, src, start=True, stop=True):
                (wa, wb), (va, vb) = wts, src
                M.matmul(o, wa, va, start=start, stop=False, skip_group_check=True)
                M.matmul(o, wa, vb, start=False, stop=False, skip_group_check=True)
                return M.matmul(o, wb, va, start=False, stop=stop, skip_group_check=True)

            def x_tiles(q):
                pe.wait_ge(s_x[q], 32)
                if q >= 2:
                    pe.wait_ge(s_xt, q - 1)
                for k in range(4):
                    last = M.transpose(ps[:, 4 + q % 2, k * P:(k + 1) * P], nat[:, 4 * q + k, :], ident[:])
                last.then_inc(s_xp, 1)

            pe.wait_ge(s_id, 1)
            pe.wait_ge(s_rnnw, 64)
            M.transpose(ps[:, 6, 0:B], cond_n[:], ident[0:B, 0:B]).then_inc(s_condp, 1)
            x_tiles(0)

            def x_part(t):
                if t % 8 == 0:
                    pe.wait_ge(s_xt, t // 8 + 1)
                M.matmul(ps[:, t % 2, 0:B], wx[:], x_f[:, t * B:(t + 1) * B], start=True, stop=False)

            def logits(q):
                if q:
                    pe.wait_ge(s_lg, q)
                else:
                    pe.wait_ge(s_rt, 32)
                for i in range(4 * q, 4 * q + 4):
                    last = M.matmul(ps[:, 2, i * GW:i * GW + E0], h_f[:, i * P:(i + 1) * P], wr[:], start=True, stop=True)
                last.then_inc(s_lgp, 1)

            def gates_turn(q):
                pe.wait_ge(s_g3, q + 1)
                if q == 0:
                    pe.wait_ge(s_id, 2)
                if q >= 2:
                    pe.wait_ge(s_gT, q - 1)
                for k in range(4):
                    at = q % 2 * C0 + k * P
                    last = M.transpose(GT_BANK[:, at:at + P], gates3[:, 4 * q + k, :], ident_b[:])
                last.then_inc(s_gTp, 1)

            x_part(0)
            for t in range(T):
                if t == 0:
                    pe.wait_ge(s_cond, 2)
                    prev = cond2[:, 0, :]
                else:
                    pe.wait_ge(s_h, t)
                    prev = h_f[:, (t - 1) * B:t * B]
                M.matmul(ps[:, t % 2, 0:B], wh[:], prev, start=False, stop=True).then_inc(s_step, 1)
                if t + 1 < T:
                    x_part(t + 1)
                if t in (1, 2, 3):
                    x_tiles(t)
                if t == 18:
                    pe.wait_ge(s_small, 16 * N_SMALL)
                    M.transpose(ps[:, 6, 128:128 + ROWS], rows[:], ident[0:ROWS, 0:ROWS]).then_inc(s_rowp, 1)
                if t == 19:
                    pe.wait_ge(s_silu, 1)
                    M.matmul(ps[:, 6, 256:256 + 2 * EC], silu2[:].rearrange("p a b -> p (a b)"), ctw_s[:],
                             start=True, stop=True).then_inc(s_modp, 1)
                if t % 8 == 0 and t:
                    logits(t // 8 - 1)
                if t % 8 == 7 and t > 8:
                    gates_turn(t // 8 - 1)
            pe.wait_ge(s_h, T)
            logits(3)

            def item0(n, i, m, first):
                e_par, j = m // J0, m % J0
                cut = slice(j * C0, (j + 1) * C0)
                e = i * 2 + e_par
                if j == 0:
                    pe.wait_ge(s_w1lo0, e + 1)
                if first and e_par == 0:
                    pe.wait_ge(s_inlo, j + 1)
                if not (first and m < 2):
                    pe.wait_ge(s_hid0, n - 1)
                mm3(bank(4 + m % 2), (w1h0[:, e_par, :], w1l0[:, e_par, :]),
                    (in_hi[:, cut], in_lo[:, cut])).then_inc(s_z0, 1)
                if first and m == 3:
                    gates_turn(3)
                if first and m < J0:
                    pe.wait_ge(s_gT, m + 1)
                if not (first and m < 2):
                    pe.wait_ge(s_hg0, n - 1)
                sel = pick_of(e)
                M.matmul(bank(6 + m % 2), sel, gates_T[:, cut], start=True, stop=True).then_inc(s_g0, 1)

            def second0(n, m, first, last):
                e_par, j = m // J0, m % J0
                cut = slice(j * C0, (j + 1) * C0)
                if first and e_par == 0:
                    pe.wait_ge(s_be2, 2)
                    for k in range(3):
                        M.matmul(bank(j), be2_p[:, k, :], gates_T[:, cut], start=k == 0, stop=False,
                                 skip_group_check=True)
                pe.wait_ge(s_lo0, n + 1)
                mm3(bank(j), (w2h0[:, e_par, :], w2l0[:, e_par, :]),
                    (hid_hi[:, m % 4, 0:C0], hid_lo[:, m % 4, 0:C0]),
                    start=False, stop=last and e_par == 1).then_inc(s_y0, 1)

            def pair0(i, first, last):
                for m in range(2 * J0):
                    item0(i * (2 * J0) + m, i, m, first)
                    if not (first and m < LAG0):
                        b = m - LAG0
                        w = b % (2 * J0)
                        if w % J0 == 0:
                            pe.wait_ge(s_w2lo0, i * 2 + (w // J0 + 1))
                        second0(i * (2 * J0) + b, w, first and b >= 0, last and b >= 0)
            pe.wait_ge(s_zero, 6)
            experts(pe, N0 // 2, pair0)
            for n in range(N_ITEMS0 - LAG0, N_ITEMS0):
                second0(n, n % (2 * J0), False, True)

            def by_bank(lo, hi):
                return [(h, max(lo, 512 * h), min(hi, 512 * (h + 1))) for h in range(2)
                        if max(lo, 512 * h) < min(hi, 512 * (h + 1))]

            def second(phase, e, n, j, f):
                item = item_base(phase, e) + n
                wbase = 0 if phase == "c" else 4 * NC_
                if j == 0 and f in (0, 2):
                    pe.wait_ge(s_wp, e * 4 + (wbase + 3 + f // 2))
                if f == 0 and not (phase == "c" and e == 0):
                    pe.wait_ge(s_yg, yg_base(phase, e) + (j - 1))
                pe.wait_ge(s_lo, item + 1)
                cut = slice(f * P, (f + 1) * P)
                for h, lo, hi in by_bank(*sees(phase, e, j)):
                    last = mm3(bank(2 * j + h)[:, lo - 512 * h:hi - 512 * h], (w2h[:, cut], w2l[:, cut]),
                               (hid_hi[:, n % 4, lo:hi], hid_lo[:, n % 4, lo:hi]), start=f == 0, stop=f == FC - 1)
                last.then_inc(s_y, 1)

            def body(phase):
                def one(e, first, last):
                    slots = SLOTS[phase, first]
                    wbase = 0 if phase == "c" else 4 * NC_
                    before = last_of(phase, e)
                    ahead = SLOTS[before[0], phase == "c" and not first and e == 1][-LAG1:]
                    line = ahead + slots
                    n_of = [2 * FC - sum(s[0] == "F" for s in ahead[k:]) for k in range(LAG1)]
                    n_of += [sum(s[0] == "F" for s in slots[:k]) for k in range(len(slots))]
                    for k, (kind, j, f) in enumerate(slots):
                        S = slot_base(phase, e) + k
                        b0 = 4 + 2 * (k % 2)
                        if not (phase == "c" and first and k < 2):
                            pe.wait_ge(s_free, S - 1)
                        if kind == "F":
                            if j == 0 and f in (0, 2):
                                pe.wait_ge(s_wp, e * 4 + (wbase + 1 + f // 2))
                            if phase == "f" and first and f == 0:
                                pe.wait_ge(s_clo, j + 1)
                            cut = slice(f * P, (f + 1) * P)
                            for h, lo, hi in by_bank(*sees(phase, e, j)):
                                if phase == "c" and first and f == 0:
                                    pe.wait_ge(s_x1lo, 2 * j + h + 1)
                                s = slice(j * C1 + lo, j * C1 + hi)
                                op = mm3(bank(b0 + h)[:, lo - 512 * h:hi - 512 * h], (w1h[:, cut], w1l[:, cut]),
                                         (in_hi[:, s], in_lo[:, s]))
                        elif kind == "G":
                            if first:
                                pe.wait_ge(s_free, slot_base(phase, 0) + slots.index(("X", 0, 0)) + 1)
                            for h in range(2):
                                s = slice(j * C1 + h * 512, j * C1 + h * 512 + 512)
                                op = M.matmul(bank(b0 + h), pick_of(e), gates_T[:, s], start=True, stop=True)
                        elif kind == "A":
                            pe.wait_ge(s_agg, 3)
                            for q in range(3):
                                op = M.matmul(ps[:, b0, 0:EC], agg[:, q, :, :].rearrange("p a b -> p (a b)"),
                                              cgw_s[:, q, :], start=q == 0, stop=q == 2)
                        elif kind == "R":
                            pe.wait_ge(s_c, 2)
                            for i in range(TILES):
                                op = M.matmul(ps[:, b0, i * EF:(i + 1) * EF], c_f[:, i * P:(i + 1) * P],
                                              cols[:, R_GF:R_GF + EF], start=True, stop=True)
                        elif phase == "c":
                            pe.wait_ge(s_gc, 1)
                            for q in range(EC):
                                op = M.matmul(ps[:, b0, q * B:(q + 1) * B], gc_w[:, q, :], ident[0:B, 0:B],
                                              start=True, stop=True)
                        else:
                            pe.wait_ge(s_g3, 5)
                            turned = pair(b0)[0:3 * GW, :].bitcast(BF16)
                            for i in range(TILES):
                                op = M.transpose(turned[:, i * P:(i + 1) * P], gates3[:, i, :], ident_b[:])
                        op.then_inc(s_full, 1)
                        kind, j, f = line[k]
                        if kind == "F" and not (phase == "c" and first and k < LAG1):
                            second(*(before if k < LAG1 else (phase, e)), n_of[k], j, f)
                return one
            for e in range(NC_):
                body("c")(e, e == 0, e == NC_ - 1)
            experts(pe, EF, body("f"))
            second("f", EF - 1, 2 * FC - 1, 1, FC - 1)

            pe.wait_ge(s_free, slot_base("f", EF))
            for j in range(J1):
                pe.wait_ge(s_fin, j + 1)
                for i in range(8):
                    op = M.transpose(ps[:, 4 + 2 * j + i // 4, (i % 4) * P:(i % 4 + 1) * P],
                                     x_f[:, (8 * j + i) * P:(8 * j + i + 1) * P], ident[:])
                op.then_inc(s_outp, 1)


_INS = ['x', 'cond_1024', 'L0_cond_Wx', 'L0_cond_Wh', 'L0_cond_b', 'L0_ffn_ws1', 'L0_ffn_bs1', 'L0_ffn_ws2',
        'L0_ffn_bs2', 'L0_ffn_We1', 'L0_ffn_Be1', 'L0_ffn_We2', 'L0_ffn_Be2', 'L0_ffn_Wr', 'L0_ffn_br',
        'L1_cond_gate_w', 'L1_cond_gate_b', 'L1_cond_time_w', 'L1_cond_time_b', 'L1_cond_ew1', 'L1_cond_eb1',
        'L1_cond_ew2', 'L1_cond_eb2', 'L1_cond_sw1', 'L1_cond_sb1', 'L1_cond_sw2', 'L1_cond_sb2',
        'L1_ffn_gate_w', 'L1_ffn_w1', 'L1_ffn_b1', 'L1_ffn_w2', 'L1_ffn_b2']


def kernel(**inputs):
    import numpy as _np
    import concourse.bacc as _bacc
    from concourse import mybir as _mybir
    from concourse.bass_utils import run_bass_kernel_spmd as _run

    nc = _bacc.Bacc("TRN2", target_bir_lowering=False, num_devices=1)
    arrays, args = {}, []
    for name in _INS:
        a = _np.ascontiguousarray(inputs[name])
        arrays[f"in_{name}_dram"] = a
        args.append(nc.dram_tensor(f"in_{name}_dram", a.shape, _mybir.dt.from_np(a.dtype), kind="ExternalInput").ap())
    args.append(nc.dram_tensor("out_0_dram", (B, T, D), F32, kind="ExternalOutput").ap())
    build(nc, *args)
    r = _run(nc, [arrays], core_ids=[0])
    return r.results[0]["out_0_dram"]
```

```python
from contextlib import ExitStack

import concourse.bass as bass
from concourse import mybir

ACT = mybir.ActivationFunctionType
ALU = mybir.AluOpType
AX = mybir.AxisListType.X
F32 = mybir.dt.float32
F32R = mybir.dt.float32r

B, T, D = 64, 32, 128
NT = B * T
P = 128
TILES = NT // P
C0 = 512
J0 = NT // C0
C1 = 1024
J1 = NT // C1
E0, K0 = 31, 3
N0 = E0 + 1
EC, KC = 4, 2
NC_ = EC + 1
EF, KF = 8, 2
FC = 4
GW = 32
T_HEAD = T_WRIST = T // 3
NEG = -3.0e38
TAKEN = 3.0e38

R_B0 = 0
R_BC = R_B0 + N0
R_BF = R_BC + NC_ * FC
R_YC = R_BF + EF * FC
R_YF = R_YC + NC_
R_GF = R_YF + EF
ROWS = R_GF + EF

F0, F1 = ([("F", j, f) for f in range(FC)] for j in range(2))
SLOTS = {("c", True): F0[:3] + [("A", 0, 0)] + F0[3:] + F1 + [("X", 0, 0)],
         ("c", False): F0 + F1,
         ("f", True): F0 + [("R", 0, 0)] + F1[:3] + [("X", 0, 0)] + F1[3:],
         ("f", False): F0 + F1}
ALL = ((0, C1), (0, C1))
SEES = [ALL, ALL, ((0, T_HEAD * B), ((T_HEAD + T_WRIST) * B - C1, C1)), ((T_HEAD * B, C1), (0, C1)), ALL]
LAG0 = 5
N_SMALL = 15
N_WC = 3 + EC
N_WF = 1 + EF
LAG1 = 2


def build(nc, x, cond, Wx, Wh, rb, ws1, bs1, ws2, bs2, We1, Be1, We2, Be2, Wr, br,
          cgw, cgb, ctw, ctb, ew1, eb1, ew2, eb2, sw1, sb1, sw2, sb2, fgw, fw1, fb1, fw2, fb2, out):
    ctx = ExitStack()
    with ctx:
        def sb(name, shape, dt):
            return ctx.enter_context(nc.sbuf_tensor(name, shape, dt))

        def sem(name):
            return ctx.enter_context(nc.semaphore(name))

        nat = sb("nat", [P, TILES, D], F32)
        c_f = sb("c_f", [P, NT], F32)
        x_f = sb("x_f", [P, NT], F32)
        h_f = sb("h_f", [P, NT], F32)
        in_hi = sb("in_hi", [P, NT], F32R)
        in_lo = sb("in_lo", [P, NT], F32R)
        raw1 = sb("raw1", [P, N0 * D], F32)
        raw2 = sb("raw2", [P, N0 * D], F32)
        rawc1 = sb("rawc1", [P, NC_ * FC * P], F32)
        rawc2 = sb("rawc2", [P, NC_ * FC * P], F32)
        w1h0 = sb("w1h0", [P, 2, D], F32R)
        w1l0 = sb("w1l0", [P, 2, D], F32R)
        w2h0 = sb("w2h0", [P, 2, D], F32R)
        w2l0 = sb("w2l0", [P, 2, D], F32R)
        w1h = sb("w1h", [P, FC * P], F32R)
        w1l = sb("w1l", [P, FC * P], F32R)
        w2h = sb("w2h", [P, FC * P], F32R)
        w2l = sb("w2l", [P, FC * P], F32R)
        hid = sb("hid", [P, 2, C1], F32)
        hid_hi = sb("hid_hi", [P, 4, C1], F32R)
        hid_lo = sb("hid_lo", [P, 4, C1], F32R)
        yg = sb("yg", [P, 2, C1], F32)
        gates_T = sb("gates_T", [GW, NT], F32)
        gb = sb("gb", [P, NT], F32)
        gates_f = sb("gates_f", [P, EF, TILES], F32)
        gates_fT = sb("gates_fT", [P, P], F32)
        gc_w = sb("gc_w", [B, EC, P], F32)
        gc_T = sb("gc_T", [P, EC, B], F32)
        gates = sb("gates", [P, TILES, GW], F32)
        g_r1 = sb("g_r1", [P, TILES, GW], F32)
        ident = sb("ident", [P, P], F32)
        lg0 = sb("lg0", [P, TILES, E0 + 9], F32)
        lgc = sb("lgc", [P, 1, 16], F32)
        lgf = sb("lgf", [P, TILES, 16], F32)
        left = sb("left", [P, TILES, E0 + 9], F32)
        top8 = sb("top8", [P, TILES, 8], F32)
        take8 = sb("take8", [P, TILES, 8], F32)
        take8c = sb("take8c", [P, 1, 8], F32)
        take8f = sb("take8f", [P, TILES, 8], F32)
        ex = sb("ex", [P, TILES, GW], F32)
        taken = sb("taken", [P, TILES, GW], F32)
        ssum = sb("ssum", [P, TILES], F32)
        rsum = sb("rsum", [P, TILES], F32)
        cond_n = sb("cond_n", [B, D], F32)
        cond2 = sb("cond2", [P, 2, B], F32)
        silu_e = sb("silu_e", [P, 2, B], F32)
        silu2 = sb("silu2", [P, 2, B], F32)
        wx = sb("wx", [D, D], F32)
        wh = sb("wh", [D, D], F32)
        rb_c = sb("rb_c", [P, 1], F32)
        wr = sb("wr", [D, E0], F32)
        br_b = sb("br_b", [P, E0], F32)
        rows = sb("rows", [ROWS, P], F32)
        cols = sb("cols", [P, ROWS], F32)
        cgw_s = sb("cgw_s", [P, 3, EC], F32)
        cgb_b = sb("cgb_b", [P, EC], F32)
        ctw_s = sb("ctw_s", [P, 2 * EC], F32)
        ctb_b = sb("ctb_b", [P, 2 * EC], F32)
        mod = sb("mod", [P, 2 * EC], F32)
        agg_s = sb("agg_s", [P, 3, B], F32)
        agg_t = sb("agg_t", [P, 3, B], F32)
        agg = sb("agg", [P, 3, 2, B], F32)
        la = sb("la", [P, EC], F32)
        wsum = sb("wsum", [P, 1], F32)
        wrec = sb("wrec", [P, 1], F32)
        wbe = sb("wbe", [P, EC], F32)
        be2 = sb("be2", [GW, D], F32)

        bias0_cur = sb("bias0_cur", [P, 2], F32)
        bias_cur = sb("bias_cur", [P, FC], F32)

        ps = ctx.enter_context(nc.psum_tensor("ps", [P, 8, 512], F32))
        bank = lambda n: ps[:, n, :]
        pair = lambda n: ps[:, n:n + 2, :].rearrange("p a b -> p (a b)")
        gt_d = nc.dram_tensor("gt_d", (GW, NT), F32, kind="Internal").ap()
        gf_d = nc.dram_tensor("gf_d", (EF, NT), F32, kind="Internal").ap()

        s_x = [sem(f"s_xq{q}") for q in range(4)]
        s_rnnw = sem("s_rnnw")
        s_rt = sem("s_rt")
        s_small = sem("s_small")
        s_w0 = sem("s_w0")
        s_wc = sem("s_wc")
        s_wf = sem("s_wf")
        s_out = sem("s_out")
        s_gd = sem("s_gd")
        s_g1 = [sem(f"s_g1q{q}") for q in range(4)]
        s_g0 = [sem(f"s_g0p{p}") for p in range(2)]
        s_gf = [sem(f"s_gf{j}") for j in range(2)]
        s_zero = sem("s_zero")
        s_id = sem("s_id")
        s_const = sem("s_const")
        s_condp = sem("s_condp")
        s_cond = sem("s_cond")
        s_xp = sem("s_xp")
        s_xt = sem("s_xt")
        s_rowp = sem("s_rowp")
        s_cols = sem("s_cols")
        s_silue = sem("s_silue")
        s_silu = sem("s_silu")
        s_modp = sem("s_modp")
        s_mod = sem("s_mod")
        s_step = sem("s_step")
        s_h = sem("s_h")
        s_inhi = sem("s_inhi")
        s_inlo = sem("s_inlo")
        s_res = sem("s_res")
        s_lgp = sem("s_lgp")
        s_lg = sem("s_lg")
        s_shift = sem("s_shift")
        s_ex = sem("s_ex")
        s_gates = sem("s_gates")
        s_gTp = sem("s_gTp")
        s_gT = sem("s_gT")
        s_v = sem("s_v")
        s_w1hi0 = sem("s_w1hi0")
        s_w1lo0 = sem("s_w1lo0")
        s_w2hi0 = sem("s_w2hi0")
        s_w2lo0 = sem("s_w2lo0")
        s_z0 = sem("s_z0")
        s_hid0 = sem("s_hid0")
        s_hg0 = sem("s_hg0")
        s_hi0 = sem("s_hi0")
        s_lo0 = sem("s_lo0")
        s_y0 = sem("s_y0")
        s_x1 = sem("s_x1")
        s_x1hi = sem("s_x1hi")
        s_x1lo = sem("s_x1lo")
        s_b0 = sem("s_b0")
        s_b = sem("s_b")
        s_wv = sem("s_wv")
        s_wp = sem("s_wp")
        s_full = sem("s_full")
        s_hid = sem("s_hid")
        s_free = sem("s_free")
        s_lo = sem("s_lo")
        s_y = sem("s_y")
        s_y_end = sem("s_y_end")
        s_yg = sem("s_yg")
        s_acc = sem("s_acc")
        s_agg = sem("s_agg")
        s_gc = sem("s_gc")
        s_c = sem("s_c")
        s_chi = sem("s_chi")
        s_clo = sem("s_clo")
        s_fin = sem("s_fin")
        s_outp = sem("s_outp")
        s_nat = sem("s_nat")

        SLOTS_C = sum(len(SLOTS["c", e == 0]) for e in range(NC_))
        ITEMS_C = NC_ * 2 * FC
        N_ITEMS0 = N0 * J0
        hid0, yg0 = (t[:].rearrange("p a (b c) -> p (a b) c", c=C0) for t in (hid, yg))
        hid_hi0, hid_lo0 = (t[:].rearrange("p a (b c) -> p (a b) c", c=C0) for t in (hid_hi, hid_lo))
        G0 = (h_f, gb)
        GC = h_f

        block = ctx.enter_context(nc.Block())
        x_v = x.rearrange("b (i s) d -> s b i d", s=2)
        out_v = out.rearrange("b (i s) d -> s b i d", s=2)

        def slot_base(phase, e):
            if isinstance(e, int) and e == 0:
                return 0 if phase == "c" else SLOTS_C
            usual, first = len(SLOTS[phase, False]), len(SLOTS[phase, True])
            return e * usual + ((0 if phase == "c" else SLOTS_C) + first - usual)

        def item_base(phase, e):
            return e * (2 * FC) + (0 if phase == "c" else ITEMS_C)

        def yg_base(phase, e):
            return e * 2 + (0 if phase == "c" else 2 * NC_)

        def experts(eng, count, body):
            body(0, True, False)
            with eng.Fori(1, count - 1) as e:
                body(e, False, False)
            body(count - 1, False, True)

        def last_of(phase, e):
            return ("c", NC_ - 1) if phase == "f" and isinstance(e, int) and e == 0 else (phase, e - 1)

        def sees(phase, e, j):
            return SEES[e][j] if phase == "c" else (0, C1)

        def acc_base(phase, e):
            return e * 2 + (0 if phase == "c" else 2 * (NC_ - 1))

        @block.sync
        def _(sp):
            def quarter(q):
                for s in range(2):
                    sp.dma_start(nat[64 * s:64 * s + 64, 4 * q:4 * q + 4, :],
                                 x_v[s, :, 4 * q:4 * q + 4, :]).then_inc(s_x[q], 16)
            sp.dma_start(cond_n[:], cond).then_inc(s_rnnw, 16)
            quarter(0)
            sp.dma_start(wh[:], Wh).then_inc(s_rnnw, 16)
            sp.dma_start(wr[:], Wr).then_inc(s_rt, 16)
            sp.dma_start(br_b[:], br.partition_broadcast(P)).then_inc(s_rt, 16)
            for q in range(1, 4):
                quarter(q)
            small = [(rows[R_B0:R_B0 + 1, :], bs1.unsqueeze(0)), (rows[R_B0 + 1:R_BC, :], Be1),
                     (rows[R_BC:R_BC + FC, :], sb1.rearrange("(c p) -> c p", p=P)),
                     (rows[R_BC + FC:R_BF, :], eb1.rearrange("e (c p) -> (e c) p", p=P)),
                     (rows[R_BF:R_YC, :], fb1.rearrange("e (c p) -> (e c) p", p=P)),
                     (rows[R_YC:R_YC + 1, :], sb2.unsqueeze(0)), (rows[R_YC + 1:R_YF, :], eb2),
                     (rows[R_YF:R_GF, :], fb2), (rows[R_GF:ROWS, :], fgw),
                     (be2[0:E0, :], Be2), (be2[E0:N0, :], bs2.unsqueeze(0)),
                     (ctw_s[:], ctw), (ctb_b[:], ctb.partition_broadcast(P)),
                     (cgw_s[:], cgw.rearrange("(k p) e -> p k e", p=P)), (cgb_b[:], cgb.partition_broadcast(P))]
            assert len(small) == N_SMALL
            for dst, src in small:
                sp.dma_start(dst, src).then_inc(s_small, 16)
            for dst, routed, shared in ((raw1, We1, ws1), (raw2, We2, ws2)):
                d = dst[:].rearrange("p (e f) -> p e f", f=D)
                sp.dma_start(d[:, 0, :], shared).then_inc(s_w0, 16)
                sp.dma_start(d[:, 1:N0, :], routed.rearrange("e k f -> k e f")).then_inc(s_w0, 16)
            d = rawc1[:].rearrange("p (e f) -> p e f", e=NC_)
            sp.dma_start(d[:, 0, :], sw1).then_inc(s_wc, 16)
            sp.dma_start(d[:, 1:NC_, :], ew1.rearrange("e k f -> k e f")).then_inc(s_wc, 16)
            d = rawc2[:].rearrange("p (e c f) -> p e c f", e=NC_, c=FC)
            sp.dma_start(d[:, 0, :, :], sw2.rearrange("(c p) f -> p c f", p=P)).then_inc(s_wc, 16)
            for e in range(EC):
                sp.dma_start(d[:, 1 + e, :, :], ew2[e].rearrange("(c p) f -> p c f", p=P)).then_inc(s_wc, 16)
            for q in range(4):
                cut = slice(q * C0, (q + 1) * C0)
                sp.wait_ge(s_gT, q + 1)
                sp.dma_start(gt_d[:, cut], gates_T[:, cut]).then_inc(s_gd, 16)
                if q == 3:
                    sp.wait_ge(s_inhi, 4)
                    sp.wait_ge(s_lgp, TILES)
                    sp.wait_ge(s_inlo, 4)
                    sp.wait_ge(s_res, 4)
                    sp.dma_start(G0[0][:, 0:3 * C0], gt_d[1:2, 0:3 * C0].broadcast_to([P, 3 * C0])
                                 ).then_inc(s_g0[0], 16)
                sp.wait_ge(s_gd, 16 * (q + 1))
                sp.dma_start(G0[1][:, cut], gt_d[0:1, cut].broadcast_to([P, C0])).then_inc(s_g1[q], 16)

            sp.dma_start(G0[0][:, 3 * C0:NT], gt_d[1:2, 3 * C0:NT].broadcast_to([P, C0])).then_inc(s_g0[0], 16)
            sp.wait_ge(s_hg0, J0)
            sp.dma_start(G0[1][:], gt_d[2:3, :].broadcast_to([P, NT])).then_inc(s_g0[1], 16)
            with sp.Fori(2, N0 // 2) as i:
                for par in range(2):
                    sp.wait_ge(s_hg0, i * (2 * J0) + (par - 2) * J0)
                    sp.dma_start(G0[par][:], gt_d[bass.ds(i * 2 + (par - 1), 1), :].broadcast_to([P, NT])
                                 ).then_inc(s_g0[par], 16)
            sp.wait_ge(s_w1lo0, N0)
            sp.wait_ge(s_w2lo0, N0)
            sp.dma_start(raw1[:].rearrange("p (e f) -> p e f", e=EF),
                         fw1.rearrange("e k f -> k e f")).then_inc(s_wf, 16)
            d = raw2[:].rearrange("p (e c f) -> p e c f", e=EF, c=FC)
            for e in range(EF):
                sp.dma_start(d[:, e, :, :], fw2[e].rearrange("(c p) f -> p c f", p=P)).then_inc(s_wf, 16)
            sp.wait_ge(s_free, SLOTS_C + SLOTS["f", True].index(("X", 0, 0)) + 1)
            sp.dma_start(gf_d.rearrange("e (i t) -> (e i) t", t=P), gates_fT[:]).then_inc(s_gd, 16)
            sp.wait_ge(s_gd, 16 * 5)

            def gates_of(e, first):
                for j in range(J1):
                    if not first:
                        sp.wait_ge(s_yg, yg_base("f", e - 1) + (j + 1))
                    cut = slice(j * C1, (j + 1) * C1)
                    sp.dma_start(GC[:, cut], gf_d[bass.ds(e, 1), cut].broadcast_to([P, C1])).then_inc(s_gf[j], 16)
            gates_of(0, True)
            with sp.Fori(1, EF) as e:
                gates_of(e, False)
            for q in range(4):
                sp.wait_ge(s_nat, q + 1)
                sp.dma_start(out_v[0, :, 4 * q:4 * q + 4, :], nat[0:64, 4 * q:4 * q + 4, :]).then_inc(s_out, 16)
            sp.wait_ge(s_out, 16 * 2 * 4)

        @block.gpsimd
        def _(pool):
            nc.gpsimd.memset(ident[:], 0.0).then_inc(s_zero, 1)
            pool.wait_ge(s_zero, 1)
            nc.gpsimd.affine_select(out=ident[:], in_=ident[:], compare_op=ALU.not_equal, fill=1.0, base=0,
                                    pattern=[[-1, P]], channel_multiplier=1).then_inc(s_id, 1)
            for tab in (lg0, take8, lgc, lgf, take8c, take8f):
                nc.gpsimd.memset(tab[:], NEG).then_inc(s_const, 1)
            nc.gpsimd.memset(gates[:, :, E0:N0], 1.0).then_inc(s_const, 1)
            nc.gpsimd.memset(c_f[:], 0.0).then_inc(s_const, 1)

            def lo0(e, par, which):
                raw, hi, lo, s_hi, s_lo = ((raw1, w1h0, w1l0, s_w1hi0, s_w1lo0),
                                           (raw2, w2h0, w2l0, s_w2hi0, s_w2lo0))[which]
                pool.wait_ge(s_hi, e + 1)
                nc.gpsimd.tensor_tensor(lo[:, par, :], raw[:, bass.ds(e * D, D)], hi[:, par, :].bitcast(F32),
                                        ALU.subtract).then_inc(s_lo, 1)
            for q in range(4):
                cut = slice(q * C0, (q + 1) * C0)
                pool.wait_ge(s_inhi, q + 1)
                nc.gpsimd.tensor_tensor(in_lo[:, cut], h_f[:, cut], in_hi[:, cut].bitcast(F32),
                                        ALU.subtract).then_inc(s_inlo, 1)
                if q == 2:
                    lo0(0, 0, 0)
                    lo0(0, 0, 1)
                    lo0(1, 1, 0)
            for q in range(4):
                cut = slice(q * C0, (q + 1) * C0)
                pool.wait_ge(s_h, T)
                nc.gpsimd.tensor_tensor(x_f[:, cut], x_f[:, cut], h_f[:, cut], ALU.add).then_inc(s_res, 1)
            lo0(1, 1, 1)
            with pool.Fori(1, N0 // 2) as i:
                lo0(i * 2, 0, 0)
                lo0(i * 2, 0, 1)
                lo0(i * 2 + 1, 1, 0)
                lo0(i * 2 + 1, 1, 1)

            def w_lo(half, e, raws, count):
                hi, lo, raw = ((w1h, w1l, raws[0]), (w2h, w2l, raws[1]))[half // 2]
                at = half % 2 * 2 * P
                pool.wait_ge(s_wv, count)
                nc.gpsimd.tensor_tensor(lo[:, at:at + 2 * P], raw[:, bass.ds(e * (FC * P) + at, 2 * P)],
                                        hi[:, at:at + 2 * P].bitcast(F32), ALU.subtract).then_inc(s_wp, 1)

            def add(phase, e, j):
                acc = c_f if phase == "c" else x_f
                lo, hi = sees(phase, e, j)
                cut = slice(j * C1 + lo, j * C1 + hi)
                pool.wait_ge(s_yg, yg_base(phase, e) + j + 1)
                nc.gpsimd.tensor_tensor(acc[:, cut], acc[:, cut], yg[:, j, lo:hi], ALU.add).then_inc(s_acc, 1)

            for half in range(4):
                w_lo(half, 0, (rawc1, rawc2), half + 1)

            def body(phase):
                raws = (rawc1, rawc2) if phase == "c" else (raw1, raw2)
                wbase = 0 if phase == "c" else 4 * NC_

                def one(e, first, last):
                    late = phase == "f" and first
                    if not (phase == "c" and first):
                        w_lo(3, e, raws, e * 4 + (wbase + 4))
                    if not first:
                        add(phase, e - 1, 1)
                    if not last and not late:
                        add(phase, e, 0)
                    if not last or phase == "c":
                        nxt, src = (0, (raw1, raw2)) if last else (e + 1, raws)
                        for half in range(3):
                            w_lo(half, nxt, src, e * 4 + (wbase + 4 + half + 1))
                    if late:
                        add(phase, e, 0)
                return one
            for e in range(NC_):
                body("c")(e, e == 0, e == NC_ - 1)
            experts(pool, EF, body("f"))

        @block.scalar
        def _(act):
            act.dma_start(wx[:], Wx).then_inc(s_rnnw, 16)
            act.dma_start(rb_c[:], rb.unsqueeze(1)).then_inc(s_rnnw, 16)
            act.wait_ge(s_cond, 2)
            nc.scalar.activation(silu_e[:], cond2[:], ACT.Exp, scale=-1.0).then_inc(s_silue, 1)

            def route_exp(q, cut, n, shifts):
                act.wait_ge(s_shift, shifts)
                nc.scalar.activation(ex[:, cut, 0:n], g_r1[:, cut, 0:n], ACT.Exp).then_inc(s_ex, 1)

            def w_hi0(par, cut, which):
                raw, hi, s = ((raw1, w1h0, s_w1hi0), (raw2, w2h0, s_w2hi0))[which]
                act.wait_ge(s_w0, 64)
                nc.scalar.activation(hi[:, par, :], raw[:, cut], ACT.Copy).then_inc(s, 1)

            act.wait_ge(s_rnnw, 64)
            for t in range(T):
                act.wait_ge(s_step, t + 1)
                nc.scalar.activation(h_f[:, t * B:(t + 1) * B], ps[:, t % 2, 0:B], ACT.Tanh,
                                     bias=rb_c[:, 0:1]).then_inc(s_h, 1)
                if t % 8 == 5 and t > 8:
                    q = t // 8 - 1
                    route_exp(q, slice(4 * q, 4 * q + 4), E0, q + 1)
                if t == T - 4:
                    w_hi0(0, slice(0, D), 0)
                    w_hi0(0, slice(0, D), 1)
                if t == T - 3:
                    w_hi0(1, slice(D, 2 * D), 0)
            route_exp(3, slice(12, 16), E0, 4)

            def item0(n, i, m, last):
                e_par, j = m // J0, m % J0
                act.wait_ge(s_z0, n + 1)
                if isinstance(n, int) and 4 <= n < J0 + 4:
                    act.wait_ge(s_lo0, n - 3)
                elif not (isinstance(n, int) and n < 4):
                    act.wait_ge(s_hg0, n - (J0 + 3))
                e = i * 2 + e_par
                if j == 0:
                    act.wait_ge(s_b0, e + 1)
                nc.scalar.activation(hid0[:, m % 4, :], bank(4 + m % 4), ACT.Gelu,
                                     bias=bias0_cur[:, e_par:e_par + 1]).then_inc(s_hid0, 1)
                if not (isinstance(n, int) and n == 0):
                    hi0(n - 1, (m - 1) % 8)
                if j == 0 and not (isinstance(n, int) and n == 0):
                    if not (isinstance(n, int) and n == J0):
                        act.wait_ge(s_y0, n - J0)
                    w_hi0(e_par, bass.ds(e * D, D), 1)
                if j == 0 and not (isinstance(n, int) and n == 0) and not (last and e_par == 1):
                    w_hi0(1 - e_par, bass.ds(e * D + D, D), 0)

            def hi0(n, m):
                if isinstance(n, int) and n < J0:
                    act.wait_ge(s_hid0, n + 1)
                    src = hid0
                else:
                    act.wait_ge(s_hg0, n - (J0 - 1))
                    src = yg0
                if not (isinstance(n, int) and n < 8):
                    act.wait_ge(s_y0, n - 7)
                nc.scalar.activation(hid_hi0[:, m % 8, :], src[:, m % 4, :], ACT.Copy).then_inc(s_hi0, 1)

            def pair0(i, first, last):
                for m in range(2 * J0):
                    item0(i * (2 * J0) + m, i, m, last)
            experts(act, N0 // 2, pair0)
            hi0(N_ITEMS0 - 1, 2 * J0 - 1)

            def x1_hi(q):
                cut = slice(q * C0, (q + 1) * C0)
                act.wait_ge(s_x1, q + 1)
                nc.scalar.activation(in_hi[:, cut], x_f[:, cut], ACT.Copy).then_inc(s_x1hi, 1)
            x1_hi(0)
            x1_hi(1)

            def c_hi(j):
                cut = slice(j * C1, (j + 1) * C1)
                act.wait_ge(s_c, j + 1)
                nc.scalar.activation(in_hi[:, cut], c_f[:, cut], ACT.Copy).then_inc(s_chi, 1)

            def body(phase):
                func = ACT.Gelu_apprx_tanh if phase == "c" else ACT.Relu

                def one(e, first, last):
                    n = 0
                    for k, (kind, j, f) in enumerate(SLOTS[phase, first]):
                        S = slot_base(phase, e) + k
                        lo, hi = sees(phase, e, j)
                        src = pair(4 + 2 * (k % 2))
                        act.wait_ge(s_full, S + 1)
                        if kind == "F":
                            item = item_base(phase, e) + n
                            bias = bias_cur[:, f:f + 1]
                            if j == 0 and f in (0, 2):
                                act.wait_ge(s_b, (e * 2 + (f // 2 + 1)) + (0 if phase == "c" else 2 * NC_))
                            if not (phase == "c" and first and n < 2):
                                act.wait_ge(s_lo, item - 1)
                            nc.scalar.activation(hid[:, n % 2, lo:hi], src[:, lo:hi], func,
                                                 bias=bias).then_inc(s_hid, 1)
                            if not (phase == "c" and first and n < 4):
                                act.wait_ge(s_y, item - 3)
                            nc.scalar.activation(hid_hi[:, n % 4, lo:hi], src[:, lo:hi], func,
                                                 bias=bias).then_inc(s_free, 1)
                            n += 1
                        elif kind == "A":
                            nc.scalar.activation(la[:], src[:, 0:EC], ACT.Copy).then_inc(s_free, 1)
                        elif kind == "R":
                            nc.scalar.activation(lgf[:, :, 0:EF],
                                                 src[:, 0:TILES * EF].rearrange("p (i e) -> p i e", e=EF),
                                                 ACT.Copy).then_inc(s_free, 1)
                        elif phase == "c":
                            nc.scalar.activation(gc_T[:].rearrange("p e b -> p (e b)"), src[:, 0:EC * B],
                                                 ACT.Copy).then_inc(s_free, 1)
                        else:
                            nc.scalar.activation(gates_fT[:], src[:, 0:P], ACT.Copy).then_inc(s_free, 1)
                        if phase == "c" and first and k == 1:
                            x1_hi(2)
                            x1_hi(3)
                        if phase == "c" and first and k == 5:
                            act.wait_ge(s_shift, 5)
                            nc.scalar.activation(ex[:, 0:1, 0:EC], g_r1[:, 0:1, 0:EC], ACT.Exp).then_inc(s_ex, 1)
                        if phase == "c" and last and k == 6:
                            c_hi(0)
                        if phase == "f" and first and k == 2:
                            c_hi(1)
                        if phase == "f" and first and k == 5:
                            act.wait_ge(s_shift, 6)
                            nc.scalar.activation(ex[:, :, 0:EF], g_r1[:, :, 0:EF], ACT.Exp).then_inc(s_ex, 1)
                return one
            for e in range(NC_):
                body("c")(e, e == 0, e == NC_ - 1)
            experts(act, EF, body("f"))
            for q in range(4):
                act.wait_ge(s_outp, q + 1)
                nc.scalar.activation(nat[:, 4 * q:4 * q + 4, :], bank(4 + q).rearrange("p (i d) -> p i d", d=D),
                                     ACT.Copy).then_inc(s_nat, 1)
                act.wait_ge(s_nat, q + 1)
                act.dma_start(out_v[1, :, 4 * q:4 * q + 4, :], nat[64:128, 4 * q:4 * q + 4, :]).then_inc(s_out, 16)

        @block.vector
        def _(dve):
            chain = [0]

            def link(ins):
                chain[0] += 1
                ins.then_inc(s_v, 1)
                dve.wait_ge(s_v, chain[0])

            V = nc.vector
            dve.wait_ge(s_condp, 1)
            V.tensor_copy(cond2[:, 0, :], ps[:, 6, 0:B]).then_inc(s_cond, 1)
            for i in range(TILES):
                dve.wait_ge(s_xp, i + 1)
                V.tensor_copy(x_f[:, i * P:(i + 1) * P], ps[:, 4 + i % 2, 0:P]).then_inc(s_xt, 1)
                if i == 0:
                    V.tensor_copy(cond2[:, 1, :], ps[:, 6, 0:B]).then_inc(s_cond, 1)
            dve.wait_ge(s_silue, 1)
            link(V.tensor_scalar(silu_e[:], silu_e[:], 1.0, None, ALU.add))
            link(V.reciprocal(silu_e[:], silu_e[:]))
            V.tensor_tensor(silu2[:], cond2[:], silu_e[:], ALU.mult).then_inc(s_silu, 1)

            def biases_and_modulation():
                dve.wait_ge(s_rowp, 1)
                V.tensor_copy(cols[:], ps[:, 6, 128:128 + ROWS]).then_inc(s_cols, 1)
                dve.wait_ge(s_small, 16 * N_SMALL)
                dve.wait_ge(s_modp, 1)
                V.tensor_tensor(mod[:], ps[:, 6, 256:256 + 2 * EC], ctb_b[:], ALU.add).then_inc(s_mod, 1)
                dve.wait_ge(s_mod, 1)
                V.tensor_scalar(mod[:, 0:EC], mod[:, 0:EC], 1.0, None, ALU.add).then_inc(s_mod, 1)

            def topk(lg, tiles, n, k, take, part, pad):
                if part == 0:
                    for i in tiles:
                        V.max(top8[:, i, :], lg[:, i, 0:max(n, 8)]).then_inc(s_v, 1)
                        chain[0] += 1
                    dve.wait_ge(s_v, chain[0])
                    cut = slice(tiles[0], tiles[-1] + 1)
                    V.tensor_tensor(g_r1[:, cut, 0:n], lg[:, cut, 0:n],
                                    top8[:, cut, 0:1].broadcast_to([P, len(tiles), n]),
                                    ALU.subtract).then_inc(s_shift, 1)
                    link(V.tensor_copy(take[:, cut, 0:k], top8[:, cut, 0:k]))
                else:
                    for i in tiles:
                        V.match_replace(left[:, i, 0:pad], take[:, i, :], lg[:, i, 0:pad], TAKEN).then_inc(s_v, 1)
                        chain[0] += 1
                    dve.wait_ge(s_v, chain[0])
                    cut = slice(tiles[0], tiles[-1] + 1)
                    link(V.tensor_tensor(taken[:, cut, 0:n], left[:, cut, 0:n], lg[:, cut, 0:n], ALU.not_equal))

            def softmax(tiles, n, exs, out_g):
                cut = slice(tiles[0], tiles[-1] + 1)
                dve.wait_ge(s_ex, exs)
                link(V.tensor_reduce(ssum[:, cut], ex[:, cut, 0:n], AX, ALU.add))
                link(V.reciprocal(rsum[:, cut], ssum[:, cut]))
                link(V.tensor_tensor(ex[:, cut, 0:n], ex[:, cut, 0:n], taken[:, cut, 0:n], ALU.mult))
                V.tensor_tensor(out_g, ex[:, cut, 0:n],
                                rsum[:, cut].unsqueeze(2).broadcast_to([P, len(tiles), n]),
                                ALU.mult).then_inc(s_gates, 1)

            def gates_T_out(q):
                dve.wait_ge(s_gTp, 4 * q + 4)
                V.tensor_copy(gates_T[:, q * C0:(q + 1) * C0], ps[0:GW, 3, :]).then_inc(s_gT, 1)

            def w_hi(half, e, raws):
                hi, raw = ((w1h, raws[0]), (w2h, raws[1]))[half // 2]
                at = half % 2 * 2 * P
                V.tensor_copy(hi[:, at:at + 2 * P], raw[:, bass.ds(e * (FC * P) + at, 2 * P)]).then_inc(s_wv, 1)

            def route0(q, part):
                tiles = list(range(4 * q, 4 * q + 4))
                if part == 0:
                    dve.wait_ge(s_lgp, 4 * q + 4)
                    V.tensor_tensor(lg0[:, 4 * q:4 * q + 4, 0:E0],
                                    ps[:, 2, 128 * q:128 * q + 128].rearrange("p (i e) -> p i e", e=GW)[:, :, 0:E0],
                                    br_b[:].unsqueeze(1).broadcast_to([P, 4, E0]), ALU.add).then_inc(s_lg, 1)
                    dve.wait_ge(s_lg, q + 1)
                    topk(lg0, tiles, E0, K0, take8, 0, 0)
                    topk(lg0, tiles, E0, K0, take8, 1, E0 + 9)
                else:
                    softmax(tiles, E0, q + 1, gates[:, 4 * q:4 * q + 4, 0:E0])

            def bias0(e, par):
                V.tensor_scalar(bias0_cur[:, par:par + 1], cols[:, bass.ds(e + R_B0, 1)], 0.0, None,
                                ALU.add).then_inc(s_b0, 1)

            def bias1(phase, e, half):
                at = e * FC + ((R_BC if phase == "c" else R_BF) + 2 * half)
                V.tensor_scalar(bias_cur[:, 2 * half:2 * half + 2], cols[:, bass.ds(at, 2)], 0.0, None,
                                ALU.add).then_inc(s_b, 1)

            dve.wait_ge(s_const, 7)
            for q in range(4):
                dve.wait_ge(s_h, 8 * q + 8)
                cut = slice(q * C0, (q + 1) * C0)
                if q < 3:
                    V.tensor_copy(in_hi[:, cut], h_f[:, cut]).then_inc(s_inhi, 1)
                route0(q, 0)
                if q == 3:
                    V.tensor_copy(in_hi[:, cut], h_f[:, cut]).then_inc(s_inhi, 1)
                route0(q, 1)
                if q:
                    gates_T_out(q - 1)
                if q == 1:
                    biases_and_modulation()
                    dve.wait_ge(s_cols, 1)
                    bias0(0, 0)
                    bias0(1, 1)
                    bias1("c", 0, 0)
                    bias1("c", 0, 1)
            dve.wait_ge(s_wc, 16 * N_WC)
            for half in range(4):
                w_hi(half, 0, (rawc1, rawc2))

            def hg0(n, i, m):
                j = m % J0
                dve.wait_ge(s_hid0, n + 1)
                if isinstance(n, int) and n < 2 * J0:
                    dve.wait_ge(s_g1[j], 16)
                elif j == 0:
                    dve.wait_ge(s_g0[m // J0], i * 16 + (16 if m == 0 else 0))
                if not (isinstance(n, int) and n < J0 + 4):
                    dve.wait_ge(s_lo0, n - 3)
                V.tensor_tensor(yg0[:, m % 4, :], hid0[:, m % 4, :], G0[m // J0][:, j * C0:(j + 1) * C0],
                                ALU.mult).then_inc(s_hg0, 1)

            def lo0(n, m):
                dve.wait_ge(s_hi0, n + 1)
                src = hid0 if isinstance(n, int) and n < J0 else yg0
                V.tensor_tensor(hid_lo0[:, m % 8, :], src[:, m % 4, :], hid_hi0[:, m % 8, :].bitcast(F32),
                                ALU.subtract).then_inc(s_lo0, 1)

            def pair0(i, first, last):
                for m in range(2 * J0):
                    n = i * (2 * J0) + m
                    if not (first and m < J0):
                        hg0(n, i, m)
                    if not (first and m == 0):
                        lo0(n - 1, (m - 1) % 8)
                    if m % J0 == 0 and not (first and m == 0) and not (last and m == J0):
                        bias0(i * 2 + (m // J0 + 1), 1 - m // J0)
            gates_T_out(3)
            experts(dve, N0 // 2, pair0)

            def x1(q):
                cut = slice(q * C0, (q + 1) * C0)
                dve.wait_ge(s_res, q + 1)
                dve.wait_ge(s_y0, N_ITEMS0 - J0 + q + 1)
                V.tensor_tensor(x_f[:, cut], x_f[:, cut], bank(q), ALU.add).then_inc(s_x1, 1)

            def x1_lo(q):
                cut = slice(q * C0, (q + 1) * C0)
                dve.wait_ge(s_x1hi, q + 1)
                V.tensor_tensor(in_lo[:, cut], x_f[:, cut], in_hi[:, cut].bitcast(F32), ALU.subtract).then_inc(s_x1lo, 1)
            x1(0)
            lo0(N_ITEMS0 - 1, 2 * J0 - 1)
            x1(1)
            x1_lo(0)
            x1(2)
            x1_lo(1)
            x1(3)

            def means(part):
                seg = x_f[:].rearrange("p (t b) -> p b t", b=B)
                cuts = (slice(0, T_HEAD), slice(T_HEAD, T_HEAD + T_WRIST), slice(T_HEAD + T_WRIST, T))
                if part < 3:
                    if part == 0:
                        dve.wait_ge(s_x1, 4)
                    V.tensor_reduce(agg_s[:, part, :], seg[:, :, cuts[part]], AX, ALU.add).then_inc(s_v, 1)
                    chain[0] += 1
                    return
                dve.wait_ge(s_v, chain[0])
                head, wrist, prop = (agg_s[:, k, :] for k in range(3))
                link(V.tensor_tensor(agg_t[:, 1, :], head, prop, ALU.add))
                link(V.tensor_tensor(agg_t[:, 2, :], wrist, prop, ALU.add))
                link(V.tensor_tensor(agg_t[:, 0, :], agg_t[:, 1, :], wrist, ALU.add))
                for k, count in enumerate((T, T - T_WRIST, T - T_HEAD)):
                    V.tensor_scalar(agg[:, k, :, :], agg_t[:, k, :].unsqueeze(1).broadcast_to([P, 2, B]),
                                    1.0 / count, None, ALU.mult).then_inc(s_agg, 1)

            def gate_c(part):
                if part == 0:
                    dve.wait_ge(s_free, SLOTS["c", True].index(("A", 0, 0)) + 1)
                    dve.wait_ge(s_mod, 2)
                    link(V.tensor_tensor(la[:], la[:], cgb_b[:], ALU.add))
                    link(V.tensor_tensor(la[:], la[:], mod[:, 0:EC], ALU.mult))
                    link(V.tensor_tensor(lgc[:, 0, 0:EC], la[:], mod[:, EC:2 * EC], ALU.add))
                    topk(lgc, [0], EC, KC, take8c, 0, 0)
                    topk(lgc, [0], EC, KC, take8c, 1, 16)
                elif part == 1:
                    softmax([0], EC, 5, wbe[:].unsqueeze(1))
                    dve.wait_ge(s_gates, 5)
                    link(V.tensor_reduce(wsum[:], wbe[:], AX, ALU.add))
                    link(V.tensor_scalar(wsum[:], wsum[:], 1e-8, None, ALU.add))
                    link(V.reciprocal(wrec[:], wsum[:]))
                    link(V.tensor_scalar(wbe[:], wbe[:], wrec[:, 0:1], None, ALU.mult))
                    V.tensor_copy(gc_w[:], wbe[0:B, :].unsqueeze(2).broadcast_to([B, EC, P])).then_inc(s_gc, 1)

            def route_f(part):
                tiles = list(range(TILES))
                if part == 0:
                    dve.wait_ge(s_free, SLOTS_C + SLOTS["f", True].index(("R", 0, 0)) + 1)
                    topk(lgf, tiles, EF, KF, take8f, 0, 0)
                elif part == 1:
                    topk(lgf, tiles, EF, KF, take8f, 1, 16)
                else:
                    softmax(tiles, EF, 6, gates_f[:].rearrange("p e i -> p i e"))

            def evac(phase, e, j):
                bias = cols[:, bass.ds(e + (R_YC if phase == "c" else R_YF), 1)]
                lo, hi = sees(phase, e, j)
                dve.wait_ge(s_y, item_base(phase, e) + (4 * j + 4))
                if phase == "c" and e == 0:
                    V.tensor_scalar(yg[:, j, lo:hi], pair(2 * j)[:, lo:hi], bias, None, ALU.add).then_inc(s_yg, 1)
                    return
                if phase == "f" and isinstance(e, int) and e == 0:
                    dve.wait_ge(s_c, 2)
                else:
                    dve.wait_ge(s_acc, acc_base(phase, e) + (j - 1))
                if phase == "c":
                    dve.wait_ge(s_free, len(SLOTS["c", True]))
                    n = (hi - lo) // B
                    V.scalar_tensor_tensor(yg[:, j, lo:hi].rearrange("p (t b) -> p t b", b=B),
                                           pair(2 * j)[:, lo:hi].rearrange("p (t b) -> p t b", b=B), bias,
                                           gc_T[:, e - 1, :].unsqueeze(1).broadcast_to([P, n, B]),
                                           ALU.add, ALU.mult).then_inc(s_yg, 1)
                    return
                dve.wait_ge(s_gf[j], e * 16 + 16)
                V.scalar_tensor_tensor(yg[:, j, :], pair(2 * j), bias, GC[:, j * C1:(j + 1) * C1],
                                       ALU.add, ALU.mult).then_inc(s_yg, 1)

            def total(phase, j):
                count = NC_ if phase == "c" else EF
                acc, s = (c_f, s_c) if phase == "c" else (x_f, s_fin)
                cut = slice(j * C1, (j + 1) * C1)
                dve.wait_ge(s_yg, yg_base(phase, count - 1) + j + 1)
                dve.wait_ge(s_acc, acc_base(phase, count - 1) + (j - 1))
                V.tensor_tensor(acc[:, cut], acc[:, cut], yg[:, j, :], ALU.add).then_inc(s, 1)

            def c_lo(j):
                cut = slice(j * C1, (j + 1) * C1)
                dve.wait_ge(s_chi, j + 1)
                V.tensor_tensor(in_lo[:, cut], c_f[:, cut], in_hi[:, cut].bitcast(F32), ALU.subtract).then_inc(s_clo, 1)

            def body(phase):
                raws = (rawc1, rawc2) if phase == "c" else (raw1, raw2)

                def one(e, first, last):
                    base = slot_base(phase, e)
                    late = phase == "f" and first
                    nxt, src = (0, (raw1, raw2)) if last else (e + 1, raws)
                    prefetch = not (last and phase == "f")
                    n = 0
                    for k, (kind, j, f) in enumerate(SLOTS[phase, first]):
                        if kind != "F":
                            continue
                        lo, hi = sees(phase, e, j)
                        dve.wait_ge(s_free, base + (k + 1))
                        V.tensor_tensor(hid_lo[:, n % 4, lo:hi], hid[:, n % 2, lo:hi],
                                        hid_hi[:, n % 4, lo:hi].bitcast(F32), ALU.subtract).then_inc(s_lo, 1)
                        n += 1
                        if (j, f) == (0, 0) and not (phase == "c" and first):
                            dve.wait_ge(s_y, item_base(phase, e))
                            w_hi(3, e, raws)
                            before = last_of(phase, e)
                            evac(*before, 1)
                        if late and (j, f) == (0, 1):
                            total("c", 1)
                        if late and (j, f) == (0, 2):
                            c_lo(1)
                        if late and (j, f) == (0, 3):
                            route_f(0)
                            route_f(1)
                        if late and (j, f) == (1, 1):
                            route_f(2)
                        if phase == "c" and first and (j, f) == (0, 0):
                            means(3)
                        if phase == "c" and first and (j, f) == (0, 3):
                            gate_c(0)
                        if phase == "c" and first and (j, f) == (0, 1):
                            x1_lo(2)
                            x1_lo(3)
                        if (j, f) == (1, 0):
                            if phase == "c" and first:
                                gate_c(1)
                            if not late:
                                evac(phase, e, 0)
                            if last and phase == "f":
                                total(phase, 0)
                        if (j, f) == (1, 1):
                            if prefetch and last:
                                dve.wait_ge(s_wf, 16 * N_WF)
                            if prefetch:
                                w_hi(0, nxt, src)
                                bias1("f" if last else phase, nxt, 0)
                            if phase == "c" and last:
                                total(phase, 0)
                        if phase == "c" and last and (j, f) == (1, 2):
                            c_lo(0)
                        if (j, f) == (1, 3) and prefetch:
                            w_hi(1, nxt, src)
                            bias1("f" if last else phase, nxt, 1)
                            dve.wait_ge(s_y, item_base(phase, e) + (4 + 2))
                            w_hi(2, nxt, src)
                    if late:
                        evac(phase, e, 0)
                    if last and phase == "f":
                        dve.wait_ge(s_acc, acc_base(phase, e))
                        dve.wait_ge(s_gf[1], e * 16 + 16)
                        for h in range(2):
                            part = slice(h * 512, (h + 1) * 512)
                            cut = slice(C1 + h * 512, C1 + (h + 1) * 512)
                            dve.wait_ge(s_y_end, h + 1)
                            link(V.scalar_tensor_tensor(yg[:, 1, part], bank(2 + h),
                                                        cols[:, R_YF + e:R_YF + e + 1], GC[:, cut],
                                                        ALU.add, ALU.mult))
                            V.tensor_tensor(x_f[:, cut], x_f[:, cut], yg[:, 1, part], ALU.add).then_inc(s_fin, 1)
                return one
            for part in range(3):
                means(part)
            for e in range(NC_):
                body("c")(e, e == 0, e == NC_ - 1)
            experts(dve, EF, body("f"))

        @block.tensor
        def _(pe):
            M = nc.tensor

            def mm3(o, wts, src, start=True, stop=True):
                (wa, wb), (va, vb) = wts, src
                M.matmul(o, wa, va, start=start, stop=False, skip_group_check=True)
                M.matmul(o, wa, vb, start=False, stop=False, skip_group_check=True)
                return M.matmul(o, wb, va, start=False, stop=stop, skip_group_check=True)

            def x_tile(i):
                if i % 4 == 0:
                    pe.wait_ge(s_x[i // 4], 32)
                if i >= 2:
                    pe.wait_ge(s_xt, i - 1)
                M.transpose(ps[:, 4 + i % 2, 0:P], nat[:, i, :], ident[:]).then_inc(s_xp, 1)

            pe.wait_ge(s_id, 1)
            for _ in range(9):
                M.matmul(ps[:, 7, 0:P], ident[:], ident[:], start=True, stop=True)
            pe.wait_ge(s_rnnw, 64)
            M.transpose(ps[:, 6, 0:B], cond_n[:], ident[0:B, 0:B]).then_inc(s_condp, 1)
            x_tile(0)
            x_tile(1)

            def x_part(t):
                if t % 2 == 0:
                    pe.wait_ge(s_xt, t // 2 + 1)
                M.matmul(ps[:, t % 2, 0:B], wx[:], x_f[:, t * B:(t + 1) * B], start=True, stop=False)

            def logits(q, k):
                if k == 0:
                    if q:
                        pe.wait_ge(s_lg, q)
                    else:
                        pe.wait_ge(s_rt, 32)
                i = 4 * q + k
                M.matmul(ps[:, 2, i * GW:i * GW + E0], h_f[:, i * P:(i + 1) * P], wr[:],
                         start=True, stop=True).then_inc(s_lgp, 1)

            def gates_turn(q, k):
                if k == 0:
                    pe.wait_ge(s_gates, q + 1)
                    if q:
                        pe.wait_ge(s_gT, q)
                M.transpose(ps[0:GW, 3, k * P:(k + 1) * P], gates[:, 4 * q + k, :], ident[:]).then_inc(s_gTp, 1)

            between = {t: [] for t in range(T + 1)}
            for k in range(3):
                between[28 + 2 * k - k // 2].append((logits, 3, k))
            for i in range(2, TILES):
                between[i // 2].append((x_tile, i))
            for k in range(4):
                for q in range(3):
                    between[8 * q + 8 + k].append((logits, q, k))
                    between[min(T, 8 * q + (16 if k == 0 else 19 + k))].append((gates_turn, q, k))
            x_part(0)
            for t in range(T):
                if t == 0:
                    pe.wait_ge(s_cond, 1)
                    prev = cond2[:, 0, :]
                else:
                    pe.wait_ge(s_h, t)
                    prev = h_f[:, (t - 1) * B:t * B]
                M.matmul(ps[:, t % 2, 0:B], wh[:], prev, start=False, stop=True).then_inc(s_step, 1)
                if t + 1 < T:
                    x_part(t + 1)
                    M.matmul(ps[:, 7, 0:P], wx[:], x_f[:, 0:P], start=True, stop=True)
                for work in between[t]:
                    work[0](*work[1:])
                if t == 18:
                    pe.wait_ge(s_small, 16 * N_SMALL)
                    M.transpose(ps[:, 6, 128:128 + ROWS], rows[:], ident[0:ROWS, 0:ROWS]).then_inc(s_rowp, 1)
                if t == 19:
                    pe.wait_ge(s_silu, 1)
                    M.matmul(ps[:, 6, 256:256 + 2 * EC], silu2[:].rearrange("p a b -> p (a b)"), ctw_s[:],
                             start=True, stop=True).then_inc(s_modp, 1)
            pe.wait_ge(s_h, T)
            logits(3, 3)
            for work in between[T]:
                work[0](*work[1:])

            def item0(n, i, m, first):
                e_par, j = m // J0, m % J0
                cut = slice(j * C0, (j + 1) * C0)
                e = i * 2 + e_par
                if j == 0:
                    pe.wait_ge(s_w1lo0, e + 1)
                if first and e_par == 0:
                    pe.wait_ge(s_inlo, j + 1)
                if first and m == 2:
                    pe.wait_ge(s_mod, 1)
                if not (first and m < 4):
                    pe.wait_ge(s_hid0, n - 3)
                mm3(bank(4 + m % 4), (w1h0[:, e_par, :], w1l0[:, e_par, :]),
                    (in_hi[:, cut], in_lo[:, cut])).then_inc(s_z0, 1)
                if first and m == 2:
                    for k in range(4):
                        gates_turn(3, k)

            def second0(n, m, e, first, last):
                e_par, j = m // J0, m % J0
                if j == 0:
                    pe.wait_ge(s_w2lo0, e + 1)
                pe.wait_ge(s_lo0, n + 1)
                mm3(bank(j), (w2h0[:, e_par, :], w2l0[:, e_par, :]),
                    (hid_hi0[:, m % 8, :], hid_lo0[:, m % 8, :]),
                    start=False, stop=last and e_par == 1).then_inc(s_y0, 1)

            def open0(j):
                pe.wait_ge(s_gT, 4 if j == 3 else j + 1)
                if j == 2:
                    pe.wait_ge(s_lg, 4)
                M.matmul(bank(j), be2[:], gates_T[:, j * C0:(j + 1) * C0], start=True, stop=False,
                         skip_group_check=True)

            def pair0(i, first, last):
                for m in range(2 * J0):
                    item0(i * (2 * J0) + m, i, m, first)
                    if first and m in (1, 3, 5):
                        for j in {1: (0, 1), 3: (2,), 5: (3,)}[m]:
                            open0(j)
                    if not (first and m < LAG0):
                        b = m - LAG0
                        second0(i * (2 * J0) + b, b % (2 * J0), i * 2 + b // J0, first and b >= 0, last and b >= 0)
            experts(pe, N0 // 2, pair0)
            for n in range(N_ITEMS0 - LAG0, N_ITEMS0):
                second0(n, n % (2 * J0), n // J0, False, True)

            def by_bank(lo, hi):
                return [(h, max(lo, 512 * h), min(hi, 512 * (h + 1))) for h in range(2)
                        if max(lo, 512 * h) < min(hi, 512 * (h + 1))]

            def second(phase, e, n, j, f):
                item = item_base(phase, e) + n
                wbase = 0 if phase == "c" else 4 * NC_
                if j == 0 and f in (0, 2):
                    pe.wait_ge(s_wp, e * 4 + (wbase + 3 + f // 2))
                if f == 0 and not (phase == "c" and e == 0):
                    pe.wait_ge(s_yg, yg_base(phase, e) + (j - 1))
                pe.wait_ge(s_lo, item + 1)
                cut = slice(f * P, (f + 1) * P)
                for h, lo, hi in by_bank(*sees(phase, e, j)):
                    last = mm3(bank(2 * j + h)[:, lo - 512 * h:hi - 512 * h], (w2h[:, cut], w2l[:, cut]),
                               (hid_hi[:, n % 4, lo:hi], hid_lo[:, n % 4, lo:hi]), start=f == 0, stop=f == FC - 1)
                    if isinstance(e, int) and (phase, e, n) == ("f", EF - 1, 2 * FC - 1):
                        last.then_inc(s_y_end, 1)
                if not (isinstance(e, int) and (phase, e, n) == ("f", EF - 1, 2 * FC - 1)):
                    last.then_inc(s_y, 1)

            def body(phase):
                def one(e, first, last):
                    slots = SLOTS[phase, first]
                    wbase = 0 if phase == "c" else 4 * NC_
                    before = last_of(phase, e)
                    n = 0
                    for k, (kind, j, f) in enumerate(slots):
                        S = slot_base(phase, e) + k
                        b0 = 4 + 2 * (k % 2)
                        if not (phase == "c" and first and k < 2):
                            pe.wait_ge(s_free, S - 1)
                        if kind == "F":
                            if j == 0 and f in (0, 2):
                                pe.wait_ge(s_wp, e * 4 + (wbase + 1 + f // 2))
                            if phase == "f" and first and f == 0:
                                pe.wait_ge(s_clo, j + 1)
                            cut = slice(f * P, (f + 1) * P)
                            for h, lo, hi in by_bank(*sees(phase, e, j)):
                                if phase == "c" and first and f == 0:
                                    pe.wait_ge(s_x1lo, 2 * j + h + 1)
                                s = slice(j * C1 + lo, j * C1 + hi)
                                op = mm3(bank(b0 + h)[:, lo - 512 * h:hi - 512 * h], (w1h[:, cut], w1l[:, cut]),
                                         (in_hi[:, s], in_lo[:, s]))
                        elif kind == "A":
                            pe.wait_ge(s_agg, 3)
                            for q in range(3):
                                op = M.matmul(ps[:, b0, 0:EC], agg[:, q, :, :].rearrange("p a b -> p (a b)"),
                                              cgw_s[:, q, :], start=q == 0, stop=q == 2)
                        elif kind == "R":
                            pe.wait_ge(s_c, 2)
                            for i in range(TILES):
                                op = M.matmul(ps[:, b0, i * EF:(i + 1) * EF], c_f[:, i * P:(i + 1) * P],
                                              cols[:, R_GF:R_GF + EF], start=True, stop=True)
                        elif phase == "c":
                            pe.wait_ge(s_gc, 1)
                            for q in range(EC):
                                op = M.matmul(ps[:, b0, q * B:(q + 1) * B], gc_w[:, q, :], ident[0:B, 0:B],
                                              start=True, stop=True)
                        else:
                            pe.wait_ge(s_gates, 6)
                            op = M.transpose(ps[:, b0, 0:P], gates_f[:].rearrange("p e i -> p (e i)"), ident[:])
                        op.then_inc(s_full, 1)
                        if kind == "F":
                            back = n - LAG1
                            if back >= 0:
                                second(phase, e, back, back // FC, back % FC)
                            elif not (phase == "c" and first):
                                second(*before, back + 2 * FC, 1, back + FC)
                            n += 1
                return one
            for e in range(NC_):
                body("c")(e, e == 0, e == NC_ - 1)
            experts(pe, EF, body("f"))

            def turn_out(q):
                pe.wait_ge(s_fin, max(1, q))
                for i in range(4):
                    op = M.transpose(ps[:, 4 + q, i * P:(i + 1) * P],
                                     x_f[:, (4 * q + i) * P:(4 * q + i + 1) * P], ident[:])
                op.then_inc(s_outp, 1)

            for k in range(LAG1):
                second("f", EF - 1, 2 * FC - LAG1 + k, 1, FC - LAG1 + k)
                if k == LAG1 - 2:
                    pe.wait_ge(s_free, slot_base("f", EF) - 1)
                    turn_out(0)
                    turn_out(1)
            pe.wait_ge(s_free, slot_base("f", EF))
            turn_out(2)
            turn_out(3)


_INS = ['x', 'cond_1024', 'L0_cond_Wx', 'L0_cond_Wh', 'L0_cond_b', 'L0_ffn_ws1', 'L0_ffn_bs1', 'L0_ffn_ws2',
        'L0_ffn_bs2', 'L0_ffn_We1', 'L0_ffn_Be1', 'L0_ffn_We2', 'L0_ffn_Be2', 'L0_ffn_Wr', 'L0_ffn_br',
        'L1_cond_gate_w', 'L1_cond_gate_b', 'L1_cond_time_w', 'L1_cond_time_b', 'L1_cond_ew1', 'L1_cond_eb1',
        'L1_cond_ew2', 'L1_cond_eb2', 'L1_cond_sw1', 'L1_cond_sb1', 'L1_cond_sw2', 'L1_cond_sb2',
        'L1_ffn_gate_w', 'L1_ffn_w1', 'L1_ffn_b1', 'L1_ffn_w2', 'L1_ffn_b2']


def kernel(**inputs):
    import numpy as _np
    import concourse.bacc as _bacc
    from concourse import mybir as _mybir
    from concourse.bass_utils import run_bass_kernel_spmd as _run

    nc = _bacc.Bacc("TRN2", target_bir_lowering=False, num_devices=1)
    arrays, args = {}, []
    for name in _INS:
        a = _np.ascontiguousarray(inputs[name])
        arrays[f"in_{name}_dram"] = a
        args.append(nc.dram_tensor(f"in_{name}_dram", a.shape, _mybir.dt.from_np(a.dtype), kind="ExternalInput").ap())
    args.append(nc.dram_tensor("out_0_dram", (B, T, D), F32, kind="ExternalOutput").ap())
    build(nc, *args)
    r = _run(nc, [arrays], core_ids=[0])
    return r.results[0]["out_0_dram"]
```
